# Optimizing a Trainium2 kernel written in Bass

```python
import numpy as np
import jax
import jax.numpy as jnp

def _softmax(x, axis=-1):
    return jax.nn.softmax(x, axis=axis)

def _gelu(x):
    return jax.nn.gelu(x, approximate=True)

def _silu(x):
    return jax.nn.silu(x)

def _sigmoid(x):
    return jax.nn.sigmoid(x)

def _layernorm(x, axis=-1, eps=1e-05):
    m = jnp.mean(x, axis=axis, keepdims=True)
    v = jnp.var(x, axis=axis, keepdims=True)
    return (x - m) / jnp.sqrt(v + eps)

def _scatter_add(tgt, idx, src, axis=0):
    return tgt.at[idx].add(src)

def _segment_sum(src, seg, n):
    return jax.ops.segment_sum(src, seg, n)
kernel_name = 'mk_macaron_d1_jaxref_r8_1c05da'

def setup_inputs(seed: int=0):
    np.random.seed(seed)
    _w = jnp.asarray

    def _L0_attn_setup():
        import jax, jax.numpy as jnp
        import numpy as np
        LR = 0.001

        def _mlp(params, h):
            W1, b1, W2, b2 = params
            return jax.nn.silu(h @ W1 + b1) @ W2 + b2
        key = jax.random.key(seed)
        ks = jax.random.split(key, 6)
        B, S, D = (8, 256, 128)
        sc = 1.0 / np.sqrt(D)
        x = jax.random.normal(ks[0], (B, S, D), dtype=jnp.float32)
        W_Q = jax.random.normal(ks[1], (D, D), dtype=jnp.float32) * sc
        W_KV = jax.random.normal(ks[2], (D, 2 * D), dtype=jnp.float32) * sc
        W1 = jax.random.normal(ks[3], (D, D), dtype=jnp.float32) * sc
        b1 = jnp.zeros((D,), dtype=jnp.float32)
        W2 = jax.random.normal(ks[4], (D, D), dtype=jnp.float32) * sc
        b2 = jnp.zeros((D,), dtype=jnp.float32)
        return {'x': x, 'W_Q': W_Q, 'W_KV': W_KV, 'W1': W1, 'b1': b1, 'W2': W2, 'b2': b2}
    _L0_attn_in = _L0_attn_setup()

    def _L0_ffn_setup():
        import jax, jax.numpy as jnp
        import numpy as np
        TOP_K = 2

        def _mlp(x, w_fc, w_proj):
            return jnp.square(jax.nn.relu(x @ w_fc.T)) @ w_proj.T
        key = jax.random.key(seed)
        ks = jax.random.split(key, 6)
        B, S, D, E = (4, 256, 128, 8)
        d_ff = 4 * D
        x = jax.random.normal(ks[0], (B, S, D), dtype=jnp.float32)
        router_w = jax.random.normal(ks[1], (E, D), dtype=jnp.float32) * 0.02
        w_fc = jax.random.normal(ks[2], (E, d_ff, D), dtype=jnp.float32) * 0.02
        w_proj = jax.random.normal(ks[3], (E, D, d_ff), dtype=jnp.float32) * 0.02
        shared_fc = jax.random.normal(ks[4], (d_ff, D), dtype=jnp.float32) * 0.02
        shared_proj = jax.random.normal(ks[5], (D, d_ff), dtype=jnp.float32) * 0.02
        return {'x': x, 'router_w': router_w, 'w_fc': w_fc, 'w_proj': w_proj, 'shared_fc': shared_fc, 'shared_proj': shared_proj}
    _L0_ffn_in = _L0_ffn_setup()
    _d = {'L0_attn_x': _L0_attn_in['x'], 'L0_attn_W_Q': _L0_attn_in['W_Q'], 'L0_attn_W_KV': _L0_attn_in['W_KV'], 'L0_attn_W1': _L0_attn_in['W1'], 'L0_attn_b1': _L0_attn_in['b1'], 'L0_attn_W2': _L0_attn_in['W2'], 'L0_attn_b2': _L0_attn_in['b2'], 'L0_ffn_router_w': _L0_ffn_in['router_w'], 'L0_ffn_w_fc': _L0_ffn_in['w_fc'], 'L0_ffn_w_proj': _L0_ffn_in['w_proj'], 'L0_ffn_shared_fc': _L0_ffn_in['shared_fc'], 'L0_ffn_shared_proj': _L0_ffn_in['shared_proj']}
    _x0 = _d['L0_attn_x']
    _d['L0_attn_x'] = jax.random.normal(jax.random.fold_in(jax.random.key(seed), 1), (2, 1024, 128), dtype=_x0.dtype)
    del _x0
    return _d

def reference(L0_attn_x, L0_attn_W_Q, L0_attn_W_KV, L0_attn_W1, L0_attn_b1, L0_attn_W2, L0_attn_b2, L0_ffn_router_w, L0_ffn_w_fc, L0_ffn_w_proj, L0_ffn_shared_fc, L0_ffn_shared_proj):

    def _L0_attn_ref(x, W_Q, W_KV, W1, b1, W2, b2):
        import jax, jax.numpy as jnp
        import numpy as np
        LR = 0.001

        def _mlp(params, h):
            W1, b1, W2, b2 = params
            return jax.nn.silu(h @ W1 + b1) @ W2 + b2
        kv = x @ W_KV
        k, v = jnp.split(kv, 2, axis=-1)
        k = jnp.swapaxes(k, 0, 1)
        v = jnp.swapaxes(v, 0, 1)

        def loss_fn(params, k_t, v_t):
            return jnp.mean((_mlp(params, k_t) - v_t) ** 2)

        def step(params, kvt):
            k_t, v_t = kvt
            g = jax.grad(loss_fn)(params, k_t, v_t)
            new_params = tuple((p - LR * gp for p, gp in zip(params, g)))
            return (new_params, None)
        params, _ = jax.lax.scan(step, (W1, b1, W2, b2), (k, v))
        q = x @ W_Q
        return _mlp(params, q)

    def _L0_ffn_ref(x, router_w, w_fc, w_proj, shared_fc, shared_proj):
        import jax, jax.numpy as jnp
        import numpy as np
        TOP_K = 2

        def _mlp(x, w_fc, w_proj):
            return jnp.square(jax.nn.relu(x @ w_fc.T)) @ w_proj.T
        B, S, D = x.shape
        E = router_w.shape[0]
        T = B * S
        flat = x.reshape(T, D)
        logits = flat @ router_w.T
        probs = jax.nn.softmax(logits.astype(jnp.float32), axis=-1)
        topk_p, topk_i = jax.lax.top_k(probs, TOP_K)
        topk_w = (topk_p / jnp.maximum(topk_p.sum(-1, keepdims=True), 1e-09)).astype(flat.dtype)
        combine = jnp.zeros((T, E), dtype=flat.dtype)
        combine = combine.at[jnp.arange(T)[:, None], topk_i].add(topk_w)
        out = jnp.zeros_like(flat)
        for e in range(E):
            out = out + _mlp(flat, w_fc[e], w_proj[e]) * combine[:, e:e + 1]
        out = out + _mlp(flat, shared_fc, shared_proj)
        return out.reshape(B, S, D)
    x = L0_attn_x
    x = x + 0.5 * _L0_ffn_ref(_layernorm(x, axis=-1), L0_ffn_router_w, L0_ffn_w_fc, L0_ffn_w_proj, L0_ffn_shared_fc, L0_ffn_shared_proj)
    x = x + _L0_attn_ref(_layernorm(x, axis=-1), L0_attn_W_Q, L0_attn_W_KV, L0_attn_W1, L0_attn_b1, L0_attn_W2, L0_attn_b2)
    x = x + 0.5 * _L0_ffn_ref(_layernorm(x, axis=-1), L0_ffn_router_w, L0_ffn_w_fc, L0_ffn_w_proj, L0_ffn_shared_fc, L0_ffn_shared_proj)
    return x

_drawn_inputs = setup_inputs


def setup_inputs(seed=0):
    import zlib

    import numpy as np

    out = dict(_drawn_inputs(seed))
    spreads = {'L0_attn_b1': (0.0, 0.1), 'L0_attn_b2': (0.0, 0.1)}
    factors = {'L0_attn_W_KV': 4.576,
     'L0_ffn_router_w': 3.979,
     'L0_ffn_w_fc': 3.785,
     'L0_ffn_w_proj': 3.454}
    for name, (base, spread) in spreads.items():
        noise = np.random.default_rng([zlib.crc32(name.encode()), seed]).standard_normal(out[name].shape)
        drawn = base * np.exp(spread * noise) if base else spread * noise
        out[name] = jnp.asarray(drawn.astype(out[name].dtype))
    for name, factor in factors.items():
        out[name] = (out[name] * factor).astype(out[name].dtype)
    return out
```

```python
from contextlib import ExitStack

import concourse.bass as bass
from concourse import mybir

ALU = mybir.AluOpType
ACT = mybir.ActivationFunctionType
AX = mybir.AxisListType
F32 = mybir.dt.float32
I32 = mybir.dt.int32
U32 = mybir.dt.uint32

P = 128
B = 2
S = 1024
T = B * S
STEPS = P // B
NBLK = T // P
GRP = 4
NG = NBLK // GRP
COLS = GRP * P
E = 8
TOPK = 2
FJ = 4
NHID = (E + 1) * FJ
BUFS = 3
ITERS = 7
TOL = 1e-5
LR = 1e-3
GRAD = LR * 2.0 / (B * P)
EPS = 1e-5


def mk_macaron(nc, x, wq, wkv, w1, b1, w2, w2t, b2, router, fc, proj, out):
    with ExitStack() as ctx:
        def sb(name, shape, dt=F32):
            return ctx.enter_context(nc.sbuf_tensor(name, shape, dt))

        def psum(name):
            return ctx.enter_context(nc.psum_tensor(name, [P, 512], F32))

        def sem(name):
            return ctx.enter_context(nc.semaphore(name))

        bank = [psum(f"bank{i}") for i in range(8)]

        res = sb("res", [P, NBLK, P])
        ln = sb("ln", [P, NBLK, P])
        ln_t = sb("ln_t", [P, T])
        fc_sb = sb("fc_sb", [P, E + 1, FJ * P])
        proj_sb = sb("proj_sb", [P, NHID, P])
        router_sb = sb("router_sb", [P, E])
        wq_sb = sb("wq_sb", [P, P])
        wkv_sb = sb("wkv_sb", [P, 2 * P])
        w1_sb = sb("w1_sb", [P, P])
        w2_sb = sb("w2_sb", [P, P])
        w2t_sb = sb("w2t_sb", [P, P])
        b1_sb = sb("b1_sb", [P, 1])
        b2_sb = sb("b2_sb", [P, 1])
        ident = sb("ident", [P, P])
        nmask = sb("nmask", [P, B, STEPS])
        rowmask = sb("rowmask", [P, STEPS])
        iota_e = sb("iota_e", [P, NBLK, E])
        ones = sb("ones", [P, 64])
        stats = sb("stats", [P, NBLK, 6])
        mv = sb("mv", [P, NBLK, 2])
        rs_x = sb("rs_x", [P, NBLK * E])
        rs_y = sb("rs_y", [P, NBLK * E])
        rs_t = sb("rs_t", [P, NBLK * E])
        logits = sb("logits", [P, NBLK, E])
        probs = sb("probs", [P, NBLK, E])
        stat1 = sb("stat1", [P, NBLK])
        stat2 = sb("stat2", [P, NBLK])
        top = sb("top", [P, NBLK, 8])
        topi = sb("topi", [P, NBLK, 8], U32)
        topif = sb("topif", [P, NBLK, 8])
        pick = sb("pick", [P, NBLK, E])
        comb = sb("comb", [P, NBLK, E])
        root = sb("root", [P, NBLK, E])
        xs = sb("xs", [P, 2, GRP, P])
        xs_t = sb("xs_t", [P, 2, COLS])
        relu = sb("relu", [P, BUFS, COLS])
        hid = sb("hid", [P, BUFS, COLS])
        out_t = sb("out_t", [P, COLS])
        unused = sb("unused", [P, 1])
        k_t = sb("k_t", [P, T])
        v_t = sb("v_t", [P, T])
        k_rows = sb("k_rows", [P, NBLK, P])
        kk = sb("kk", [P, NBLK, P])
        krow_now = sb("krow_now", [P, P])
        v_now = sb("v_now", [P, P])
        sg = sb("sg", [P, P])
        a_t = sb("a_t", [P, P])
        a_rows = sb("a_rows", [P, P])
        aa = sb("aa", [P, P])
        e_t = sb("e_t", [P, P])
        e_rows = sb("e_rows", [P, 2, P])
        ee = sb("ee", [P, P])
        slope_u = sb("slope_u", [P, P])
        slope_v = sb("slope_v", [P, P])
        slope = sb("slope", [P, P])
        slope_rows = sb("slope_rows", [P, P])
        d_rows = sb("d_rows", [P, 2, P])
        gap = sb("gap", [P, 4, P])
        gap_sq = sb("gap_sq", [P, 4, P])
        gap_sum = sb("gap_sum", [P, 4, P])
        norms = sb("norms", [P, 4])
        nrm = sb("nrm", [1, 4])
        good = sb("good", [1, 2])
        n_good = sb("n_good", [1, 1])
        flag = sb("flag", [1, 1], I32)

        x_in = sem("x_in")
        weights_in = sem("weights_in")
        consts_made = sem("consts_made")
        dve_step = sem("dve_step")
        pool_step = sem("pool_step")
        ln_done = sem("ln_done")
        lnT_done = sem("lnT_done")
        lnT_copied = sem("lnT_copied")
        logits_done = sem("logits_done")
        shifted_done = sem("shifted_done")
        exp_done = sem("exp_done")
        root_done = sem("root_done")
        xs_done = sem("xs_done")
        xsT_done = sem("xsT_done")
        xsT_copied = sem("xsT_copied")
        hid_mm_done = sem("hid_mm_done")
        relu_done = sem("relu_done")
        hid_done = sem("hid_done")
        out_mm_done = sem("out_mm_done")
        outT_copied = sem("outT_copied")
        out_rows_done = sem("out_rows_done")
        res_done = sem("res_done")
        kv_mm_done = sem("kv_mm_done")
        kv_copied = sem("kv_copied")
        kk_mm_done = sem("kk_mm_done")
        kk_done = sem("kk_done")
        krows_copied = sem("krows_copied")
        kcol_done = sem("kcol_done")
        vcol_done = sem("vcol_done")
        kT_done = sem("kT_done")
        know_done = sem("know_done")
        vnow_done = sem("vnow_done")
        h_done = sem("h_done")
        sg_done = sem("sg_done")
        a_done = sem("a_done")
        y_done = sem("y_done")
        aT_done = sem("aT_done")
        arows_done = sem("arows_done")
        aa_mm_done = sem("aa_mm_done")
        aa_done = sem("aa_done")
        e_done = sem("e_done")
        ee_mm_done = sem("ee_mm_done")
        ee_done = sem("ee_done")
        eT_done = sem("eT_done")
        erows_done = sem("erows_done")
        slope_done = sem("slope_done")
        slopeT_done = sem("slopeT_done")
        sloperows_done = sem("sloperows_done")
        da_done = sem("da_done")
        d_done = sem("d_done")
        upd_done = sem("upd_done")
        params_done = sem("params_done")
        gap_done = sem("gap_done")
        gap_step = sem("gap_step")
        norms_done = sem("norms_done")
        s_step = sem("s_step")
        s_eT = sem("s_eT")
        qy_done = sem("qy_done")
        total_done = sem("total_done")
        flag_done = sem("flag_done")
        params_in = sem("params_in")
        s_know = sem("s_know")
        s_h = sem("s_h")
        s_sg = sem("s_sg")
        s_a = sem("s_a")
        s_y = sem("s_y")
        s_aT = sem("s_aT")
        s_arows = sem("s_arows")
        s_e = sem("s_e")
        s_da = sem("s_da")
        s_slope = sem("s_slope")
        s_slopeT = sem("s_slopeT")
        s_sloperows = sem("s_sloperows")
        s_ed = sem("s_ed")
        s_upd = sem("s_upd")
        s_params = sem("s_params")
        q_done = sem("q_done")
        q_copied = sem("q_copied")
        qh_done = sem("qh_done")
        qsg_done = sem("qsg_done")
        qa_done = sem("qa_done")
        stored = sem("stored")

        def dve_link(dve, ins, at):
            at[0] += 1
            ins.then_inc(dve_step, 1)
            dve.wait_ge(dve_step, at[0])

        def silu_rest(dst, pre, bias, gate):
            return nc.vector.scalar_tensor_tensor(dst, pre, bias, gate, ALU.add, ALU.mult)

        def col(block):
            return bass.ds(block * P, P)

        def rsqrt(dve, at, n):
            X, Y, Z = rs_x[:, 0:n], rs_y[:, 0:n], rs_t[:, 0:n]
            dve_link(dve, nc.vector.tensor_scalar(Z.bitcast(I32), X.bitcast(I32), 1, None, ALU.logical_shift_right), at)
            dve_link(dve, nc.vector.tensor_scalar(Y.bitcast(I32), Z.bitcast(I32), -1.0, float(0x5F3759DF),
                                                  ALU.mult, ALU.add), at)
            for _ in range(4):
                dve_link(dve, nc.vector.tensor_tensor(Z, X, Y, ALU.mult), at)
                dve_link(dve, nc.vector.scalar_tensor_tensor(Z, Z, -0.5, Y, ALU.mult, ALU.mult), at)
                dve_link(dve, nc.vector.scalar_tensor_tensor(Y, Z, 1.5, Y, ALU.add, ALU.mult), at)

        def layernorm(dve, at):
            for b in range(NBLK):
                last = nc.vector.bn_stats(stats[:, b, :], res[:, b, :])
            dve_link(dve, last, at)
            for b in range(NBLK):
                last = nc.vector.bn_aggr(mv[:, b, :], stats[:, b, :])
            dve_link(dve, last, at)
            dve_link(dve, nc.vector.tensor_scalar(rs_x[:, 0:NBLK], mv[:, :, 1], EPS, None, ALU.add), at)
            rsqrt(dve, at, NBLK)
            for b in range(NBLK):
                nc.vector.tensor_scalar(ln[:, b, :], res[:, b, :], mv[:, b, 0:1], rs_y[:, b:b + 1],
                                        ALU.subtract, ALU.mult).then_inc(ln_done, 1)

        def route(dve, at, f):
            n3 = [P, NBLK, E]
            dve.wait_ge(logits_done, f + 1)
            dve_link(dve, nc.vector.tensor_copy(logits[:], bank[6][:, 0:NBLK * E]
                                                .rearrange("p (b e) -> p b e", e=E)), at)
            dve_link(dve, nc.vector.tensor_reduce(stat1[:], logits[:], AX.X, ALU.max), at)
            nc.vector.tensor_tensor(logits[:], logits[:], stat1[:].unsqueeze(2).to_broadcast(n3),
                                    ALU.subtract).then_inc(shifted_done, 1)
            dve.wait_ge(exp_done, f + 1)
            dve_link(dve, nc.vector.tensor_reduce(stat1[:], probs[:], AX.X, ALU.add), at)
            dve_link(dve, nc.vector.reciprocal(stat2[:], stat1[:]), at)
            dve_link(dve, nc.vector.tensor_tensor(probs[:], probs[:], stat2[:].unsqueeze(2).to_broadcast(n3),
                                                  ALU.mult), at)
            for b in range(NBLK):
                last = nc.vector.max(top[:, b, :], probs[:, b, :])
            dve_link(dve, last, at)
            for b in range(NBLK):
                last = nc.vector.max_index(topi[:, b, :], top[:, b, :], probs[:, b, :])
            dve_link(dve, last, at)
            dve_link(dve, nc.vector.tensor_copy(topif[:], topi[:]), at)
            dve_link(dve, nc.vector.tensor_tensor(stat1[:], top[:, :, 0], top[:, :, 1], ALU.add), at)
            dve_link(dve, nc.vector.tensor_scalar(stat1[:], stat1[:], 1e-9, None, ALU.max), at)
            dve_link(dve, nc.vector.reciprocal(stat2[:], stat1[:]), at)
            dve_link(dve, nc.vector.tensor_tensor(top[:], top[:], stat2[:].unsqueeze(2).to_broadcast(n3),
                                                  ALU.mult), at)
            for k in range(TOPK):
                dst = pick if k else comb
                dve_link(dve, nc.vector.tensor_tensor(dst[:], iota_e[:], topif[:, :, k:k + 1].to_broadcast(n3),
                                                      ALU.is_equal), at)
                dve_link(dve, nc.vector.tensor_tensor(dst[:], dst[:], top[:, :, k:k + 1].to_broadcast(n3),
                                                      ALU.mult), at)
            flat = comb[:].rearrange("p b e -> p (b e)")
            dve_link(dve, nc.vector.tensor_tensor(comb[:], comb[:], pick[:], ALU.add), at)
            dve_link(dve, nc.vector.tensor_copy(rs_x[:], flat), at)
            rsqrt(dve, at, NBLK * E)
            nc.vector.tensor_tensor(root[:].rearrange("p b e -> p (b e)"), flat, rs_y[:],
                                    ALU.mult).then_inc(root_done, 1)

        def add_out_rows(dve, u, g):
            dve.wait_ge(out_rows_done, u + 2)
            r = res[:].rearrange("p b d -> p (b d)")[:, bass.ds(g * COLS, COLS)]
            return nc.vector.tensor_tensor(r, r, bank[5][:], ALU.add).then_inc(res_done, 1)

        def load_params(eng, done):
            for dst, src in ((w1_sb, w1), (w2_sb, w2), (w2t_sb, w2t), (b1_sb, b1.rearrange("(p a) -> p a", a=1)),
                             (b2_sb, b2.rearrange("(p a) -> p a", a=1))):
                eng.dma_start(dst[:], src).then_inc(done, 16)

        def pe_ln_transposes(pe, f):
            for g in range(NG):
                n = f * NG + g
                if n >= 2:
                    pe.wait_ge(lnT_copied, n - 1)
                pe.wait_ge(ln_done, f * NBLK + (g + 1) * GRP)
                for b in range(GRP):
                    last = nc.tensor.transpose(bank[g % 2][:, b * P:(b + 1) * P], ln[:, g * GRP + b, :], ident[:])
                last.then_inc(lnT_done, 1)

        def pe_ffn(pe, f, layer):
            pe_ln_transposes(pe, layer)
            pe.wait_ge(lnT_copied, (layer + 1) * NG)
            for b in range(NBLK):
                last = nc.tensor.matmul(bank[6][:, b * E:(b + 1) * E], ln_t[:, b * P:(b + 1) * P], router_sb[:],
                                        start=True, stop=True)
            last.then_inc(logits_done, 1)
            with pe.Fori(0, NG) as g:
                n0 = (g + f * NG) * NHID

                def project(m):
                    pe.wait_ge(hid_done, n0 + (BUFS + m + 1))
                    if m == 0:
                        pe.wait_ge(outT_copied, g + (f * 2 * NG + 1))
                    last = nc.tensor.matmul(bank[3][:], proj_sb[:, m, :], hid[:, m % BUFS, :],
                                            start=(m == 0), stop=(m == NHID - 1))
                    last.then_inc(out_mm_done, 1)

                for k in range(E + 1):
                    if k:
                        pe.wait_ge(xsT_copied, g * E + f * NG * E + k)
                    for j in range(FJ):
                        m = k * FJ + j
                        rhs = xs_t[:, k % 2, :] if k else ln_t[:, bass.ds(g * COLS, COLS)]
                        pe.wait_ge(relu_done, n0 + m + 1)
                        nc.tensor.matmul(bank[m % BUFS][:], fc_sb[:, k, j * P:(j + 1) * P], rhs,
                                         start=True, stop=True).then_inc(hid_mm_done, 1)
                        if m >= 2:
                            project(m - 2)
                        if j == 1 and k < E:
                            pe.wait_ge(xs_done, g * E + f * NG * E + k + 1)
                            for b in range(GRP):
                                last = nc.tensor.transpose(bank[4][:, b * P:(b + 1) * P], xs[:, (k + 1) % 2, b, :],
                                                           ident[:])
                            last.then_inc(xsT_done, 1)
                project(NHID - 2)
                project(NHID - 1)
                pe_out_rows(pe, g + f * 2 * NG)

        def pe_out_rows(pe, u):
            pe.wait_ge(outT_copied, u + 2)
            pe.wait_ge(res_done, u + 1)
            for b in range(GRP):
                last = nc.tensor.transpose(bank[5][:, b * P:(b + 1) * P], out_t[:, b * P:(b + 1) * P], ident[:])
            last.then_inc(out_rows_done, 1)

        def act_ffn(act, f, layer):
            for g in range(NG):
                n = layer * NG + g
                act.wait_ge(lnT_done, n + 1)
                nc.scalar.copy(ln_t[:, g * COLS:(g + 1) * COLS], bank[g % 2][:]).then_inc(lnT_copied, 1)
            act.wait_ge(shifted_done, f + 1)
            nc.scalar.activation(probs[:], logits[:], ACT.Exp).then_inc(exp_done, 1)
            with act.Fori(0, NG) as g:
                n0 = (g + f * NG) * NHID
                for m in range(NHID):
                    k, j = divmod(m, FJ)
                    act.wait_ge(hid_mm_done, n0 + m + 1)
                    act.wait_ge(hid_done, n0 + m + 1)
                    nc.scalar.activation(relu[:, m % BUFS, :], bank[m % BUFS][:], ACT.Relu).then_inc(relu_done, 1)
                    if j == 2 and k < E:
                        act.wait_ge(xsT_done, g * E + (f * NG * E + k + 1 + 2))
                        nc.scalar.copy(xs_t[:, (k + 1) % 2, :], bank[4][:]).then_inc(xsT_copied, 1)
                act.wait_ge(out_mm_done, n0 + (NHID + BUFS))
                act.wait_ge(out_rows_done, g + (f * 2 * NG + 1))
                nc.scalar.mul(out_t[:], bank[3][:], 0.5).then_inc(outT_copied, 1)

        block = ctx.enter_context(nc.Block())

        @block.sync
        def _(sp):
            for b in range(B):
                sp.dma_start(res[b * STEPS:(b + 1) * STEPS, :, :],
                             x[b].rearrange("(c t) d -> t c d", t=STEPS)).then_inc(x_in, 16)
            for dst, src in ((router_sb, router), (fc_sb, fc), (proj_sb, proj), (wkv_sb, wkv), (wq_sb, wq)):
                sp.dma_start(dst[:], src).then_inc(weights_in, 16)
            load_params(sp, params_in)
            sp.wait_ge(flag_done, 1)
            ok = sp.value_load(flag[0:1, 0:1], min_val=0, max_val=1)
            with sp.If(ok == 0):
                load_params(sp, params_in)
            sp.wait_ge(res_done, 3 * NG + 1)
            for b in range(B):
                sp.dma_start(out[b].rearrange("(c t) d -> t c d", t=STEPS),
                             res[b * STEPS:(b + 1) * STEPS, :, :]).then_inc(stored, 16)
            sp.wait_ge(stored, 16 * B)

        @block.gpsimd
        def _(pool):
            pool.sem_inc(gap_done, 1)
            nc.gpsimd.memset(ident[:], 0.0)
            nc.gpsimd.memset(nmask[:], -1.0)
            nc.gpsimd.memset(rowmask[:], 0.0)
            nc.gpsimd.memset(gap_sum[:], 0.0)
            nc.gpsimd.memset(ones[:], 1.0).then_inc(consts_made, 1)
            pool.wait_ge(consts_made, 1)
            nc.gpsimd.iota(iota_e[:], pattern=[[0, NBLK], [1, E]], base=0, channel_multiplier=0,
                           allow_small_or_imprecise_dtypes=True)
            nc.gpsimd.affine_select(out=ident[:], in_=ident[:], compare_op=ALU.not_equal, fill=1.0, base=0,
                                    pattern=[[-1, P]], channel_multiplier=1).then_inc(consts_made, 1)
            for b in range(B):
                h = slice(b * STEPS, (b + 1) * STEPS)
                pool.wait_ge(consts_made, 2 + b)
                nc.gpsimd.affine_select(out=nmask[h], in_=nmask[h], compare_op=ALU.is_gt, fill=0.0, base=0,
                                        pattern=[[0, B], [1, STEPS]], channel_multiplier=-1)
                nc.gpsimd.affine_select(out=rowmask[h], in_=rowmask[h], compare_op=ALU.not_equal, fill=1.0,
                                        base=0, pattern=[[-1, STEPS]], channel_multiplier=1)\
                  .then_inc(consts_made, 1)
            pool.wait_ge(consts_made, 2 + B)

            def ffn(f):
                pool.wait_ge(root_done, f + 1)
                with pool.Fori(0, NG) as g:
                    for k in range(E):
                        pool.wait_ge(xsT_done, g * E + (f * NG * E + k + 1))
                        nc.gpsimd.tensor_tensor(xs[:, (k + 1) % 2], ln[:, bass.ds(g * GRP, GRP), :],
                                                root[:, bass.ds(g * GRP, GRP), k:k + 1].to_broadcast([P, GRP, P]),
                                                ALU.mult).then_inc(xs_done, 1)

            ffn(0)
            with pool.Fori(0, NBLK) as c:
                for i in range(ITERS):
                    pool.wait_ge(a_done, c * ITERS + (i + 1))
                    nc.gpsimd.tensor_tensor(slope_u[:], a_t[:], sg[:], ALU.mult)
                    nc.gpsimd.tensor_tensor(slope_v[:], a_t[:], sg[:], ALU.add).then_inc(pool_step, 1)
                    pool.wait_ge(pool_step, c * ITERS + (i + 1))
                    nc.gpsimd.tensor_tensor(slope[:], slope_v[:], slope_u[:], ALU.subtract).then_inc(slope_done, 1)
                new, old = (ITERS - 1) % 2, ITERS % 2
                pool.wait_ge(erows_done, (c + 1) * ITERS)
                pool.wait_ge(d_done, (c + 1) * ITERS)
                nc.gpsimd.tensor_tensor(gap[:, 3, :], d_rows[:, new, :], d_rows[:, old, :], ALU.subtract)
                nc.gpsimd.tensor_tensor(gap[:, 2, :], e_rows[:, new, :], e_rows[:, old, :], ALU.subtract)
                nc.gpsimd.tensor_copy(gap[:, 0, :], e_rows[:, new, :])
                nc.gpsimd.tensor_copy(gap[:, 1, :], d_rows[:, new, :]).then_inc(gap_done, 1)
                pool.wait_ge(gap_done, c + 2)
                nc.gpsimd.tensor_tensor(gap_sq[:], gap[:], gap[:], ALU.mult).then_inc(gap_step, 1)
                pool.wait_ge(gap_step, 2 * c + 1)
                nc.gpsimd.tensor_tensor(gap_sum[:], gap_sum[:], gap_sq[:], ALU.add).then_inc(gap_step, 1)
                pool.wait_ge(gap_step, 2 * c + 2)
            ffn(1)

        @block.scalar
        def _(act):
            act.sem_inc(relu_done, BUFS)
            act.sem_inc(outT_copied, 1)
            act_ffn(act, 0, 0)

            for g in range(NG):
                act.wait_ge(lnT_done, NG + g + 1)
                nc.scalar.copy(ln_t[:, g * COLS:(g + 1) * COLS], bank[g % 2][:]).then_inc(lnT_copied, 1)
            for g in range(NG):
                act.wait_ge(kv_mm_done, 2 * g + 1)
                nc.scalar.copy(k_t[:, g * COLS:(g + 1) * COLS], bank[g % 2 * 2][:]).then_inc(kcol_done, 1)
            for g in range(NG):
                act.wait_ge(kT_done, g + 1)
                nc.scalar.copy(k_rows[:, g * GRP:(g + 1) * GRP, :].rearrange("p b d -> p (b d)"),
                               bank[4 + g % 2][:]).then_inc(krows_copied, 1)
            act.wait_ge(krows_copied, NG)
            act.wait_ge(params_in, 16 * 5)
            nc.scalar.activation(unused[:], k_rows[:, 0, 0:1], ACT.Sigmoid)
            with act.Fori(0, NBLK) as c:
                act.wait_ge(upd_done, 5 * c + 1)
                nc.scalar.copy(krow_now[:], k_rows[:, bass.ds(c, 1), :].rearrange("p a d -> p (a d)"))\
                  .then_inc(know_done, 1)
                for i in range(ITERS):
                    n1 = c * ITERS + (i + 1)
                    act.wait_ge(h_done, n1)
                    nc.scalar.activation(sg[:], bank[0][:, 0:P], ACT.Sigmoid, bias=b1_sb[:]).then_inc(sg_done, 1)
                    act.wait_ge(aT_done, n1)
                    nc.scalar.copy(a_rows[:], bank[5][:, 0:P]).then_inc(arows_done, 1)
                    act.wait_ge(eT_done, n1)
                    if i < 2:
                        act.wait_ge(gap_done, c + 1)
                    nc.scalar.copy(e_rows[:, i % 2, :], bank[6][:, 0:P]).then_inc(erows_done, 1)
                    act.wait_ge(slopeT_done, n1)
                    nc.scalar.copy(slope_rows[:], bank[7][:, 0:P]).then_inc(sloperows_done, 1)

            act.wait_ge(flag_done, 1)
            ok = act.value_load(flag[0:1, 0:1], min_val=0, max_val=1)
            with act.If(ok == 0):
                act.wait_ge(params_in, 16 * 10)
                with act.Fori(0, NBLK) as c:
                    act.wait_ge(s_upd, c * STEPS + 1)
                    nc.scalar.copy(krow_now[:], k_rows[:, bass.ds(c, 1), :].rearrange("p a d -> p (a d)"))\
                      .then_inc(s_know, 1)
                    with act.Fori(0, STEPS) as t:
                        n1 = c * STEPS + t + 1
                        act.wait_ge(s_h, n1)
                        nc.scalar.activation(sg[:], bank[0][:, 0:P], ACT.Sigmoid, bias=b1_sb[:]).then_inc(s_sg, 1)
                        act.wait_ge(s_aT, n1)
                        nc.scalar.copy(a_rows[:], bank[5][:, 0:P]).then_inc(s_arows, 1)
                        act.wait_ge(s_slopeT, n1)
                        nc.scalar.copy(slope_rows[:], bank[7][:, 0:P]).then_inc(s_sloperows, 1)
                act.wait_ge(s_params, 5 * S + 1)

            with act.Fori(0, NG) as g:
                act.wait_ge(q_done, g + 1)
                nc.scalar.copy(xs_t[:, 0, :], bank[0][:]).then_inc(q_copied, 1)
                act.wait_ge(qh_done, g + 1)
                nc.scalar.activation(relu[:, 0, :], bank[1][:], ACT.Sigmoid, bias=b1_sb[:]).then_inc(qsg_done, 1)
                act.wait_ge(qy_done, g + 1)
                act.wait_ge(out_rows_done, g + (NG + 1))
                nc.scalar.activation(out_t[:], bank[3][:], ACT.Identity, bias=b2_sb[:]).then_inc(outT_copied, 1)
            act_ffn(act, 1, 2)

        @block.vector
        def _(dve):
            at = [0]
            dve.sem_inc(hid_done, BUFS)
            for starts_at_1 in (res_done, params_done, s_params):
                dve.sem_inc(starts_at_1, 1)

            def ffn(f, layer):
                layernorm(dve, at)
                route(dve, at, f)
                with dve.Fori(0, NG) as g:
                    n0 = (g + f * NG) * NHID
                    for m in range(NHID):
                        dve.wait_ge(relu_done, n0 + (m + 1 + BUFS))
                        dve.wait_ge(out_mm_done, n0 + (m + 1))
                        nc.vector.tensor_tensor(hid[:, m % BUFS, :], relu[:, m % BUFS, :], relu[:, m % BUFS, :],
                                                ALU.mult).then_inc(hid_done, 1)
                    add_out_rows(dve, g + f * 2 * NG, g)

            dve.wait_ge(x_in, 16 * B)
            dve.wait_ge(consts_made, 2 + B)
            ffn(0, 0)
            dve.wait_ge(res_done, NG + 1)
            layernorm(dve, at)

            for g in range(NG):
                dve.wait_ge(kv_mm_done, 2 * g + 2)
                nc.vector.tensor_copy(v_t[:, g * COLS:(g + 1) * COLS], bank[g % 2 * 2 + 1][:]).then_inc(vcol_done, 1)
            for g in range(NG):
                dve.wait_ge(kk_mm_done, g + 1)
                nc.vector.scalar_tensor_tensor(
                    kk[:, g * GRP:(g + 1) * GRP, :], bank[6 + g % 2][:].rearrange("p (b d) -> p b d", d=P), 1.0,
                    nmask[:].rearrange("p b t -> p (b t)").unsqueeze(1).to_broadcast([P, GRP, P]),
                    ALU.add, ALU.mult).then_inc(kk_done, 1)
            dve.wait_ge(vcol_done, NG)
            dve.wait_ge(params_in, 16 * 5)
            mask = nmask[:].rearrange("p b t -> p (b t)")

            def update(params, signal):
                for w, sums, count in params:
                    dve.wait_ge(upd_done if signal is params_done else s_upd, count)
                    nc.vector.tensor_tensor(w, w, sums, ALU.subtract).then_inc(signal, 1)

            with dve.Fori(0, NBLK) as c:
                dve.wait_ge(params_done, 5 * c + 1)
                nc.vector.tensor_scalar(v_now[:], v_t[:, col(c)], b2_sb[:], GRAD, ALU.subtract,
                                        ALU.mult).then_inc(vnow_done, 1)
                dve.wait_ge(vnow_done, c + 1)
                for i in range(ITERS):
                    n1 = c * ITERS + (i + 1)
                    dve.wait_ge(sg_done, n1)
                    silu_rest(a_t[:], bank[0][:, 0:P], b1_sb[:], sg[:]).then_inc(a_done, 1)
                    dve.wait_ge(y_done, n1)
                    nc.vector.scalar_tensor_tensor(e_t[:], bank[1][:, 0:P], GRAD, v_now[:], ALU.mult,
                                                   ALU.subtract).then_inc(e_done, 1)
                    if i < ITERS - 1:
                        dve.wait_ge(aa_mm_done, c * (ITERS - 1) + (i + 1))
                        nc.vector.scalar_tensor_tensor(aa[:], bank[3][:, 0:P], 1.0, mask, ALU.add,
                                                       ALU.mult).then_inc(aa_done, 1)
                    dve.wait_ge(ee_mm_done, n1)
                    nc.vector.tensor_tensor(ee[:], bank[4][:, 0:P], mask, ALU.mult).then_inc(ee_done, 1)
                    dve.wait_ge(da_done, n1)
                    dve.wait_ge(sloperows_done, n1)
                    if i < 2:
                        dve.wait_ge(gap_done, c + 1)
                    nc.vector.tensor_tensor(d_rows[:, i % 2, :], bank[2][:, 0:P], slope_rows[:],
                                            ALU.mult).then_inc(d_done, 1)
                update(((w2_sb[:], bank[3][:, 0:P], 5 * c + 2), (w2t_sb[:], bank[4][:, 0:P], 5 * c + 3),
                        (b2_sb[:], bank[6][:, 0:1], 5 * c + 4), (w1_sb[:], bank[0][:, 0:P], 5 * c + 5),
                        (b1_sb[:], bank[5][:, 0:1], 5 * c + 6)), params_done)

            dve.wait_ge(gap_step, 2 * NBLK)
            nc.vector.tensor_reduce(norms[:], gap_sum[:], AX.X, ALU.add).then_inc(norms_done, 1)
            dve.wait_ge(total_done, 1)
            dve_link(dve, nc.vector.tensor_copy(nrm[:], bank[7][0:1, 0:4]), at)
            dve_link(dve, nc.vector.scalar_tensor_tensor(good[:], nrm[:, 0:2], TOL * TOL, nrm[:, 2:4],
                                                         ALU.mult, ALU.is_ge), at)
            dve_link(dve, nc.vector.tensor_tensor(n_good[:], good[:, 0:1], good[:, 1:2], ALU.mult), at)
            dve.wait_ge(params_done, 5 * NBLK + 1)
            nc.vector.tensor_copy(flag[:], n_good[:]).then_inc(flag_done, 1)

            dve.wait_ge(flag_done, 1)
            ok = dve.value_load(flag[0:1, 0:1], min_val=0, max_val=1)
            with dve.If(ok == 0):
                dve.wait_ge(params_in, 16 * 10)
                with dve.Fori(0, NBLK) as c:
                    with dve.Fori(0, STEPS) as t:
                        n = c * STEPS + t
                        own = rowmask[:, bass.ds(t, 1)]
                        dve.wait_ge(s_params, 5 * n + 1)
                        nc.vector.tensor_scalar(v_now[:], v_t[:, col(c)], b2_sb[:], GRAD, ALU.subtract,
                                                ALU.mult).then_inc(s_step, 1)
                        dve.wait_ge(s_step, 3 * n + 1)
                        dve.wait_ge(s_sg, n + 1)
                        silu_rest(a_t[:], bank[0][:, 0:P], b1_sb[:], sg[:]).then_inc(s_a, 1)
                        dve.wait_ge(s_y, n + 1)
                        nc.vector.scalar_tensor_tensor(e_t[:], bank[1][:, 0:P], GRAD, v_now[:], ALU.mult,
                                                       ALU.subtract).then_inc(s_e, 1)
                        dve.wait_ge(s_a, n + 1)
                        nc.vector.scalar_tensor_tensor(slope_u[:], sg[:], 1.0, a_t[:], ALU.subtract,
                                                       ALU.mult).then_inc(s_step, 1)
                        dve.wait_ge(s_step, 3 * n + 2)
                        nc.vector.tensor_tensor(slope[:], sg[:], slope_u[:], ALU.subtract).then_inc(s_slope, 1)
                        dve.wait_ge(s_eT, n + 1)
                        nc.vector.tensor_scalar(e_rows[:, 0, :], bank[6][:, 0:P], own, None,
                                                ALU.mult).then_inc(s_ed, 1)
                        dve.wait_ge(s_da, n + 1)
                        dve.wait_ge(s_sloperows, n + 1)
                        nc.vector.tensor_tensor(d_rows[:, 1, :], bank[2][:, 0:P], slope_rows[:],
                                                ALU.mult).then_inc(s_step, 1)
                        dve.wait_ge(s_step, 3 * n + 3)
                        nc.vector.tensor_scalar(d_rows[:, 0, :], d_rows[:, 1, :], own, None,
                                                ALU.mult).then_inc(s_ed, 1)
                        update(((w2_sb[:], bank[3][:, 0:P], n + 2), (w2t_sb[:], bank[4][:, 0:P], n + 2),
                                (b2_sb[:], bank[6][:, 0:1], n + 2), (w1_sb[:], bank[0][:, 0:P], n + 2),
                                (b1_sb[:], bank[5][:, 0:1], n + 2)), s_params)
                dve.wait_ge(s_params, 5 * S + 1)

            with dve.Fori(0, NG) as g:
                dve.wait_ge(qsg_done, g + 1)
                silu_rest(hid[:, 0, :], bank[1][:], b1_sb[:], relu[:, 0, :]).then_inc(qa_done, 1)
                add_out_rows(dve, g + NG, g)
            dve.wait_ge(res_done, 2 * NG + 1)
            ffn(1, 2)

        @block.tensor
        def _(pe):
            pe.sem_inc(out_mm_done, BUFS)
            pe.sem_inc(xsT_done, 2)
            for starts_at_1 in (out_rows_done, upd_done, s_upd):
                pe.sem_inc(starts_at_1, 1)
            pe.wait_ge(consts_made, 2 + B)
            pe.wait_ge(weights_in, 16 * 5)
            pe_ffn(pe, 0, 0)

            pe_ln_transposes(pe, 1)
            for g in range(NG):
                pe.wait_ge(lnT_copied, NG + g + 1)
                if g == 0:
                    pe.wait_ge(lnT_copied, 2 * NG)
                if g >= 2:
                    pe.wait_ge(kcol_done, g - 1)
                    pe.wait_ge(vcol_done, g - 1)
                for part in range(2):
                    nc.tensor.matmul(bank[g % 2 * 2 + part][:], wkv_sb[:, part * P:(part + 1) * P],
                                     ln_t[:, g * COLS:(g + 1) * COLS], start=True, stop=True).then_inc(kv_mm_done, 1)
            for g in range(NG):
                pe.wait_ge(kcol_done, g + 1)
                if g >= 2:
                    pe.wait_ge(krows_copied, g - 1)
                    pe.wait_ge(kk_done, g - 1)
                for b in range(GRP):
                    block_t = k_t[:, (g * GRP + b) * P:(g * GRP + b + 1) * P]
                    last = nc.tensor.transpose(bank[4 + g % 2][:, b * P:(b + 1) * P], block_t, ident[:])
                last.then_inc(kT_done, 1)
                for b in range(GRP):
                    block_t = k_t[:, (g * GRP + b) * P:(g * GRP + b + 1) * P]
                    last = nc.tensor.matmul(bank[6 + g % 2][:, b * P:(b + 1) * P], block_t, block_t,
                                            start=True, stop=True)
                last.then_inc(kk_mm_done, 1)
            pe.wait_ge(kk_done, NG)
            pe.wait_ge(krows_copied, NG)
            pe.wait_ge(vcol_done, NG)
            pe.wait_ge(params_in, 16 * 5)

            def mm(out_bank, lhs_t, rhs, start=True, stop=True):
                return nc.tensor.matmul(out_bank[:, 0:P], lhs_t, rhs, start=start, stop=stop)

            with pe.Fori(0, NBLK) as c:
                for i in range(ITERS):
                    n1 = c * ITERS + (i + 1)
                    new, old = i % 2, (i + 1) % 2
                    if i == 0:
                        pe.wait_ge(params_done, 5 * c + 1)
                        mm(bank[0], w1_sb[:], k_t[:, col(c)]).then_inc(h_done, 1)
                    else:
                        mm(bank[0], w1_sb[:], k_t[:, col(c)], stop=False)
                        pe.wait_ge(erows_done, c * ITERS + i)
                        pe.wait_ge(aa_done, c * (ITERS - 1) + i)
                        mm(bank[1], e_rows[:, old, :], aa[:], stop=False)
                        pe.wait_ge(d_done, c * ITERS + i)
                        mm(bank[0], d_rows[:, old, :], kk[:, bass.ds(c, 1), :].rearrange("p a d -> p (a d)"),
                           start=False).then_inc(h_done, 1)
                    pe.wait_ge(a_done, n1)
                    mm(bank[1], w2_sb[:], a_t[:], start=(i == 0)).then_inc(y_done, 1)
                    nc.tensor.transpose(bank[5][:, 0:P], a_t[:], ident[:]).then_inc(aT_done, 1)
                    if i < ITERS - 1:
                        mm(bank[3], a_t[:], a_t[:]).then_inc(aa_mm_done, 1)
                    pe.wait_ge(e_done, n1)
                    mm(bank[4], e_t[:], e_t[:]).then_inc(ee_mm_done, 1)
                    mm(bank[2], e_t[:], w2t_sb[:], stop=False)
                    nc.tensor.transpose(bank[6][:, 0:P], e_t[:], ident[:]).then_inc(eT_done, 1)
                    pe.wait_ge(slope_done, n1)
                    nc.tensor.transpose(bank[7][:, 0:P], slope[:], ident[:]).then_inc(slopeT_done, 1)
                    pe.wait_ge(arows_done, n1)
                    pe.wait_ge(ee_done, n1)
                    mm(bank[2], ee[:], a_rows[:], start=False).then_inc(da_done, 1)
                e_last, d_last = e_rows[:, (ITERS - 1) % 2, :], d_rows[:, (ITERS - 1) % 2, :]
                pe.wait_ge(erows_done, (c + 1) * ITERS)
                mm(bank[3], a_rows[:], e_last).then_inc(upd_done, 1)
                mm(bank[4], e_last, a_rows[:]).then_inc(upd_done, 1)
                nc.tensor.matmul(bank[6][:, 0:1], e_last, ones[:, 0:1], start=True, stop=True).then_inc(upd_done, 1)
                pe.wait_ge(know_done, c + 1)
                pe.wait_ge(d_done, (c + 1) * ITERS)
                mm(bank[0], krow_now[:], d_last).then_inc(upd_done, 1)
                nc.tensor.matmul(bank[5][:, 0:1], d_last, ones[:, 0:1], start=True, stop=True).then_inc(upd_done, 1)

            pe.wait_ge(norms_done, 1)
            nc.tensor.matmul(bank[7][0:1, 0:4], ones[:, 0:1], norms[:], start=True, stop=True).then_inc(total_done, 1)
            pe.wait_ge(flag_done, 1)
            ok = pe.value_load(flag[0:1, 0:1], min_val=0, max_val=1)
            with pe.If(ok == 0):
                pe.wait_ge(params_in, 16 * 10)
                with pe.Fori(0, NBLK) as c:
                    with pe.Fori(0, STEPS) as t:
                        pe.wait_ge(s_know, c + 1)
                        n = c * STEPS + t
                        pe.wait_ge(s_params, 5 * n + 1)
                        mm(bank[0], w1_sb[:], k_t[:, col(c)]).then_inc(s_h, 1)
                        pe.wait_ge(s_a, n + 1)
                        mm(bank[1], w2_sb[:], a_t[:]).then_inc(s_y, 1)
                        nc.tensor.transpose(bank[5][:, 0:P], a_t[:], ident[:]).then_inc(s_aT, 1)
                        pe.wait_ge(s_e, n + 1)
                        mm(bank[2], e_t[:], w2t_sb[:]).then_inc(s_da, 1)
                        nc.tensor.transpose(bank[6][:, 0:P], e_t[:], ident[:]).then_inc(s_eT, 1)
                        pe.wait_ge(s_slope, n + 1)
                        nc.tensor.transpose(bank[7][:, 0:P], slope[:], ident[:]).then_inc(s_slopeT, 1)
                        pe.wait_ge(s_arows, n + 1)
                        pe.wait_ge(s_ed, 2 * n + 2)
                        mm(bank[3], a_rows[:], e_rows[:, 0, :])
                        mm(bank[4], e_rows[:, 0, :], a_rows[:])
                        nc.tensor.matmul(bank[6][:, 0:1], e_rows[:, 0, :], ones[:, 0:1], start=True, stop=True)
                        mm(bank[0], krow_now[:], d_rows[:, 0, :])
                        nc.tensor.matmul(bank[5][:, 0:1], d_rows[:, 0, :], ones[:, 0:1], start=True,
                                         stop=True).then_inc(s_upd, 1)
                pe.wait_ge(s_params, 5 * S + 1)

            with pe.Fori(0, NG) as g:
                nc.tensor.matmul(bank[0][:], wq_sb[:], ln_t[:, bass.ds(g * COLS, COLS)],
                                 start=True, stop=True).then_inc(q_done, 1)
                pe.wait_ge(q_copied, g + 1)
                nc.tensor.matmul(bank[1][:], w1_sb[:], xs_t[:, 0, :], start=True, stop=True).then_inc(qh_done, 1)
                pe.wait_ge(qa_done, g + 1)
                nc.tensor.matmul(bank[3][:], w2_sb[:], hid[:, 0, :], start=True, stop=True).then_inc(qy_done, 1)
                pe_out_rows(pe, g + NG)
            pe_ffn(pe, 1, 2)


def kernel(**inputs):
    import numpy as np
    import concourse.bacc as bacc
    from concourse.bass_utils import run_bass_kernel_spmd

    a = {n: np.asarray(v) for n, v in inputs.items()}
    fc = np.concatenate([a["L0_ffn_shared_fc"][None], a["L0_ffn_w_fc"]], 0)
    proj = np.concatenate([a["L0_ffn_shared_proj"][None], a["L0_ffn_w_proj"]], 0)
    arrays = {
        "x": a["L0_attn_x"],
        "wq": a["L0_attn_W_Q"],
        "wkv": a["L0_attn_W_KV"],
        "w1": a["L0_attn_W1"],
        "b1": a["L0_attn_b1"],
        "w2": a["L0_attn_W2"],
        "w2t": a["L0_attn_W2"].T,
        "b2": a["L0_attn_b2"],
        "router": a["L0_ffn_router_w"].T,
        "fc": fc.transpose(2, 0, 1),
        "proj": proj.reshape(E + 1, P, FJ, P).transpose(3, 0, 2, 1).reshape(P, NHID, P),
    }
    arrays = {n: np.ascontiguousarray(v) for n, v in arrays.items()}
    nc = bacc.Bacc("TRN2", target_bir_lowering=False, num_devices=1)
    args = {n: nc.dram_tensor(n, v.shape, mybir.dt.from_np(v.dtype), kind="ExternalInput").ap()
            for n, v in arrays.items()}
    out = nc.dram_tensor("out", (B, S, P), F32, kind="ExternalOutput").ap()
    mk_macaron(nc, out=out, **args)
    r = run_bass_kernel_spmd(nc, [arrays], core_ids=[0])
    return r.results[0]["out"]
```

```python
from contextlib import ExitStack

import concourse.bass as bass
from concourse import mybir

ALU = mybir.AluOpType
ACT = mybir.ActivationFunctionType
AX = mybir.AxisListType
F32 = mybir.dt.float32
I32 = mybir.dt.int32
U32 = mybir.dt.uint32

P = 128
B = 2
S = 1024
T = B * S
STEPS = P // B
NBLK = T // P
GRP = 4
NG = NBLK // GRP
COLS = GRP * P
E = 8
TOPK = 2
FJ = 4
NHID = (E + 1) * FJ
BUFS = 3
PAIR = 2
NPAIR = NBLK // PAIR
PCOLS = PAIR * P
PBUFS = 6
PBANKS = 2
PLAG = 4
ITERS = 7
PASSES = PAIR * ITERS
FILL = 50
TOL = 1e-5
LR = 1e-3
GRAD = LR * 2.0 / (B * P)
EPS = 1e-5


def mk_macaron(nc, x, wq, wkv, w1, b1, w2, w2t, b2, router, fc, proj, out):
    with ExitStack() as ctx:
        def sb(name, shape, dt=F32):
            return ctx.enter_context(nc.sbuf_tensor(name, shape, dt))

        def psum(name):
            return ctx.enter_context(nc.psum_tensor(name, [P, 512], F32))

        def sem(name):
            return ctx.enter_context(nc.semaphore(name))

        bank = [psum(f"bank{i}") for i in range(8)]

        res = sb("res", [P, NBLK, P])
        ln = sb("ln", [P, NBLK, P])
        ln_t = sb("ln_t", [P, T])
        fc_sb = sb("fc_sb", [P, E + 1, FJ * P])
        proj_sb = sb("proj_sb", [P, NHID, P])
        router_sb = sb("router_sb", [P, E])
        wq_sb = sb("wq_sb", [P, P])
        wkv_sb = sb("wkv_sb", [P, 2 * P])
        w1_sb = sb("w1_sb", [P, P])
        w2_sb = sb("w2_sb", [P, P])
        w2t_sb = sb("w2t_sb", [P, P])
        b1_sb = sb("b1_sb", [P, 1])
        b2_sb = sb("b2_sb", [P, 1])
        ident = sb("ident", [P, P])
        nmask = sb("nmask", [P, B, STEPS])
        rowmask = sb("rowmask", [P, STEPS])
        iota_e = sb("iota_e", [P, NBLK, E])
        ones = sb("ones", [P, 64])
        stats = sb("stats", [P, NBLK, 6])
        mv = sb("mv", [P, NBLK, 2])
        rs_x = sb("rs_x", [P, NBLK * E])
        rs_y = sb("rs_y", [P, NBLK * E])
        rs_t = sb("rs_t", [P, NBLK * E])
        logits = sb("logits", [P, NBLK, E])
        probs = sb("probs", [P, NBLK, E])
        stat1 = sb("stat1", [P, NBLK])
        stat2 = sb("stat2", [P, NBLK])
        top = sb("top", [P, NBLK, 8])
        topi = sb("topi", [P, NBLK, 8], U32)
        topif = sb("topif", [P, NBLK, 8])
        pick = sb("pick", [P, NBLK, E])
        comb = sb("comb", [P, NBLK, E])
        root = sb("root", [P, NBLK, E])
        ln1 = sb("ln1", [P, PAIR, P])
        k_new = sb("k_new", [P, PCOLS])
        xs = sb("xs", [P, 2, GRP, P])
        xs_t = sb("xs_t", [P, 2, COLS])
        relu = sb("relu", [P, BUFS, COLS])
        hid = sb("hid", [P, BUFS, COLS])
        relu_p = relu[:].rearrange("p b (a n) -> p (b a) n", n=PCOLS)
        hid_p = hid[:].rearrange("p b (a n) -> p (b a) n", n=PCOLS)
        out_t = sb("out_t", [P, COLS])
        unused = sb("unused", [P, 1])
        k_t = sb("k_t", [P, T])
        v_t = sb("v_t", [P, T])
        k_rows = sb("k_rows", [P, NBLK, P])
        kk = sb("kk", [P, NBLK, P])
        krow_now = sb("krow_now", [P, P])
        v_now = sb("v_now", [P, P])
        sg = sb("sg", [P, P])
        a_t = sb("a_t", [P, P])
        a_rows = sb("a_rows", [P, P])
        aa = sb("aa", [P, P])
        e_t = sb("e_t", [P, P])
        es_rows = sb("es_rows", [P, 2, 2, P])
        ee = sb("ee", [P, P])
        slope_u = sb("slope_u", [P, P])
        slope_v = sb("slope_v", [P, P])
        slope = sb("slope", [P, P])
        d_rows = sb("d_rows", [P, 2, P])
        gap = sb("gap", [P, 4, P])
        gap_sq = sb("gap_sq", [P, 4, P])
        gap_sum = sb("gap_sum", [P, 4, P])
        norms = sb("norms", [P, 4])
        nrm = sb("nrm", [1, 4])
        good = sb("good", [1, 2])
        n_good = sb("n_good", [1, 1])
        flag = sb("flag", [1, 1], I32)

        x_in = sem("x_in")
        weights_in = sem("weights_in")
        consts_made = sem("consts_made")
        dve_step = sem("dve_step")
        pool_step = sem("pool_step")
        ln_done = sem("ln_done")
        lnT_done = sem("lnT_done")
        lnT_copied = sem("lnT_copied")
        logits_done = sem("logits_done")
        shifted_done = sem("shifted_done")
        exp_done = sem("exp_done")
        root_done = sem("root_done")
        xs_done = sem("xs_done")
        xsT_done = sem("xsT_done")
        xsT_copied = sem("xsT_copied")
        hid_mm_done = sem("hid_mm_done")
        relu_done = sem("relu_done")
        hid_done = sem("hid_done")
        out_mm_done = sem("out_mm_done")
        outT_copied = sem("outT_copied")
        out_rows_done = sem("out_rows_done")
        res_done = sem("res_done")
        p_xs_done = sem("p_xs_done")
        p_xsT_done = sem("p_xsT_done")
        p_xsT_copied = sem("p_xsT_copied")
        p_hid_mm_done = sem("p_hid_mm_done")
        p_relu_done = sem("p_relu_done")
        p_hid_done = sem("p_hid_done")
        p_out_mm_done = sem("p_out_mm_done")
        p_outT_copied = sem("p_outT_copied")
        p_out_rows_done = sem("p_out_rows_done")
        p_norm_step = sem("p_norm_step")
        ln1_done = sem("ln1_done")
        ln1T_done = sem("ln1T_done")
        ln1T_copied = sem("ln1T_copied")
        kv_mm_done = sem("kv_mm_done")
        kk_mm_done = sem("kk_mm_done")
        kk_done = sem("kk_done")
        krows_copied = sem("krows_copied")
        kcol_done = sem("kcol_done")
        kcopy_done = sem("kcopy_done")
        vcol_done = sem("vcol_done")
        kT_done = sem("kT_done")
        know_done = sem("know_done")
        vnow_done = sem("vnow_done")
        h_done = sem("h_done")
        sg_done = sem("sg_done")
        a_done = sem("a_done")
        y_done = sem("y_done")
        aT_done = sem("aT_done")
        arows_done = sem("arows_done")
        aa_mm_done = sem("aa_mm_done")
        aa_done = sem("aa_done")
        e_done = sem("e_done")
        ee_mm_done = sem("ee_mm_done")
        ee_done = sem("ee_done")
        esT_done = sem("esT_done")
        esrows_done = sem("esrows_done")
        slope_done = sem("slope_done")
        da_done = sem("da_done")
        d_done = sem("d_done")
        upd_done = sem("upd_done")
        params_done = sem("params_done")
        gap_done = sem("gap_done")
        gap_step = sem("gap_step")
        norms_done = sem("norms_done")
        s_step = sem("s_step")
        s_eT = sem("s_eT")
        qy_done = sem("qy_done")
        total_done = sem("total_done")
        flag_done = sem("flag_done")
        params_in = sem("params_in")
        s_know = sem("s_know")
        s_h = sem("s_h")
        s_sg = sem("s_sg")
        s_a = sem("s_a")
        s_y = sem("s_y")
        s_aT = sem("s_aT")
        s_arows = sem("s_arows")
        s_e = sem("s_e")
        s_da = sem("s_da")
        s_slope = sem("s_slope")
        s_slopeT = sem("s_slopeT")
        s_sloperows = sem("s_sloperows")
        s_ed = sem("s_ed")
        s_upd = sem("s_upd")
        s_params = sem("s_params")
        q_done = sem("q_done")
        q_copied = sem("q_copied")
        qh_done = sem("qh_done")
        qsg_done = sem("qsg_done")
        qa_done = sem("qa_done")
        stored = sem("stored")

        def dve_link(dve, ins, at):
            at[0] += 1
            ins.then_inc(dve_step, 1)
            dve.wait_ge(dve_step, at[0])

        def silu_rest(dst, pre, bias, gate):
            return nc.vector.scalar_tensor_tensor(dst, pre, bias, gate, ALU.add, ALU.mult)

        def col(block):
            return bass.ds(block * P, P)

        def rsqrt(dve, at, n):
            X, Y, Z = rs_x[:, 0:n], rs_y[:, 0:n], rs_t[:, 0:n]
            dve_link(dve, nc.vector.tensor_scalar(Z.bitcast(I32), X.bitcast(I32), 1, None, ALU.logical_shift_right), at)
            dve_link(dve, nc.vector.tensor_scalar(Y.bitcast(I32), Z.bitcast(I32), -1.0, float(0x5F3759DF),
                                                  ALU.mult, ALU.add), at)
            for _ in range(4):
                dve_link(dve, nc.vector.tensor_tensor(Z, X, Y, ALU.mult), at)
                dve_link(dve, nc.vector.scalar_tensor_tensor(Z, Z, -0.5, Y, ALU.mult, ALU.mult), at)
                dve_link(dve, nc.vector.scalar_tensor_tensor(Y, Z, 1.5, Y, ALU.add, ALU.mult), at)

        def layernorm(dve, at):
            for b in range(NBLK):
                last = nc.vector.bn_stats(stats[:, b, :], res[:, b, :])
            dve_link(dve, last, at)
            for b in range(NBLK):
                last = nc.vector.bn_aggr(mv[:, b, :], stats[:, b, :])
            dve_link(dve, last, at)
            dve_link(dve, nc.vector.tensor_scalar(rs_x[:, 0:NBLK], mv[:, :, 1], EPS, None, ALU.add), at)
            rsqrt(dve, at, NBLK)
            for b in range(NBLK):
                nc.vector.tensor_scalar(ln[:, b, :], res[:, b, :], mv[:, b, 0:1], rs_y[:, b:b + 1],
                                        ALU.subtract, ALU.mult).then_inc(ln_done, 1)

        def route(dve, at, f):
            n3 = [P, NBLK, E]
            dve.wait_ge(logits_done, f + 1)
            dve_link(dve, nc.vector.tensor_copy(logits[:], bank[6][:, 0:NBLK * E]
                                                .rearrange("p (b e) -> p b e", e=E)), at)
            dve_link(dve, nc.vector.tensor_reduce(stat1[:], logits[:], AX.X, ALU.max), at)
            nc.vector.tensor_tensor(logits[:], logits[:], stat1[:].unsqueeze(2).to_broadcast(n3),
                                    ALU.subtract).then_inc(shifted_done, 1)
            dve.wait_ge(exp_done, f + 1)
            dve_link(dve, nc.vector.tensor_reduce(stat1[:], probs[:], AX.X, ALU.add), at)
            dve_link(dve, nc.vector.reciprocal(stat2[:], stat1[:]), at)
            dve_link(dve, nc.vector.tensor_tensor(probs[:], probs[:], stat2[:].unsqueeze(2).to_broadcast(n3),
                                                  ALU.mult), at)
            for b in range(NBLK):
                last = nc.vector.max(top[:, b, :], probs[:, b, :])
            dve_link(dve, last, at)
            for b in range(NBLK):
                last = nc.vector.max_index(topi[:, b, :], top[:, b, :], probs[:, b, :])
            dve_link(dve, last, at)
            dve_link(dve, nc.vector.tensor_copy(topif[:], topi[:]), at)
            dve_link(dve, nc.vector.tensor_tensor(stat1[:], top[:, :, 0], top[:, :, 1], ALU.add), at)
            dve_link(dve, nc.vector.tensor_scalar(stat1[:], stat1[:], 1e-9, None, ALU.max), at)
            dve_link(dve, nc.vector.reciprocal(stat2[:], stat1[:]), at)
            dve_link(dve, nc.vector.tensor_tensor(top[:], top[:], stat2[:].unsqueeze(2).to_broadcast(n3),
                                                  ALU.mult), at)
            for k in range(TOPK):
                dst = pick if k else comb
                dve_link(dve, nc.vector.tensor_tensor(dst[:], iota_e[:], topif[:, :, k:k + 1].to_broadcast(n3),
                                                      ALU.is_equal), at)
                dve_link(dve, nc.vector.tensor_tensor(dst[:], dst[:], top[:, :, k:k + 1].to_broadcast(n3),
                                                      ALU.mult), at)
            flat = comb[:].rearrange("p b e -> p (b e)")
            dve_link(dve, nc.vector.tensor_tensor(comb[:], comb[:], pick[:], ALU.add), at)
            dve_link(dve, nc.vector.tensor_copy(rs_x[:], flat), at)
            rsqrt(dve, at, NBLK * E)
            nc.vector.tensor_tensor(root[:].rearrange("p b e -> p (b e)"), flat, rs_y[:],
                                    ALU.mult).then_inc(root_done, 1)

        def add_out_rows(dve, u, g):
            dve.wait_ge(out_rows_done, u + 2)
            r = res[:].rearrange("p b d -> p (b d)")[:, bass.ds(g * COLS, COLS)]
            return nc.vector.tensor_tensor(r, r, bank[5][:], ALU.add).then_inc(res_done, 1)

        def load_params(eng, done):
            for dst, src in ((w1_sb, w1), (w2_sb, w2), (w2t_sb, w2t), (b1_sb, b1.rearrange("(p a) -> p a", a=1)),
                             (b2_sb, b2.rearrange("(p a) -> p a", a=1))):
                eng.dma_start(dst[:], src).then_inc(done, 16)

        def pe_ln_transposes(pe, f):
            for g in range(NG):
                n = f * NG + g
                if n >= 2:
                    pe.wait_ge(lnT_copied, n - 1)
                pe.wait_ge(ln_done, f * NBLK + (g + 1) * GRP)
                for b in range(GRP):
                    last = nc.tensor.transpose(bank[g % 2][:, b * P:(b + 1) * P], ln[:, g * GRP + b, :], ident[:])
                last.then_inc(lnT_done, 1)

        def pe_route(pe, f):
            pe_ln_transposes(pe, f)
            pe.wait_ge(lnT_copied, (f + 1) * NG)
            for b in range(NBLK):
                last = nc.tensor.matmul(bank[6][:, b * E:(b + 1) * E], ln_t[:, b * P:(b + 1) * P], router_sb[:],
                                        start=True, stop=True)
            last.then_inc(logits_done, 1)

        def pe_ffn(pe):
            with pe.Fori(0, NG) as g:
                n0 = g * NHID

                def project(m):
                    pe.wait_ge(hid_done, n0 + (BUFS + m + 1))
                    if m == 0:
                        pe.wait_ge(outT_copied, g + (NG + 1))
                    last = nc.tensor.matmul(bank[3][:], proj_sb[:, m, :], hid[:, m % BUFS, :],
                                            start=(m == 0), stop=(m == NHID - 1))
                    last.then_inc(out_mm_done, 1)

                for k in range(E + 1):
                    if k:
                        pe.wait_ge(xsT_copied, g * E + k)
                    for j in range(FJ):
                        m = k * FJ + j
                        rhs = xs_t[:, k % 2, :] if k else ln_t[:, bass.ds(g * COLS, COLS)]
                        pe.wait_ge(relu_done, n0 + m + 1)
                        nc.tensor.matmul(bank[m % BUFS][:], fc_sb[:, k, j * P:(j + 1) * P], rhs,
                                         start=True, stop=True).then_inc(hid_mm_done, 1)
                        if m >= 2:
                            project(m - 2)
                        if j == 1 and k < E:
                            pe.wait_ge(xs_done, g * E + (k + 1))
                            for b in range(GRP):
                                last = nc.tensor.transpose(bank[4][:, b * P:(b + 1) * P], xs[:, (k + 1) % 2, b, :],
                                                           ident[:])
                            last.then_inc(xsT_done, 1)
                project(NHID - 2)
                project(NHID - 1)
                pe_out_rows(pe, g + NG)

        def pe_out_rows(pe, u):
            pe.wait_ge(outT_copied, u + 2)
            pe.wait_ge(res_done, u + 1)
            for b in range(GRP):
                last = nc.tensor.transpose(bank[5][:, b * P:(b + 1) * P], out_t[:, b * P:(b + 1) * P], ident[:])
            last.then_inc(out_rows_done, 1)

        def act_ffn(act, f):
            for g in range(NG):
                n = f * NG + g
                act.wait_ge(lnT_done, n + 1)
                nc.scalar.copy(ln_t[:, g * COLS:(g + 1) * COLS], bank[g % 2][:]).then_inc(lnT_copied, 1)
            act.wait_ge(shifted_done, f + 1)
            nc.scalar.activation(probs[:], logits[:], ACT.Exp).then_inc(exp_done, 1)
            if f == 0:
                return
            with act.Fori(0, NG) as g:
                n0 = g * NHID
                for m in range(NHID):
                    k, j = divmod(m, FJ)
                    act.wait_ge(hid_mm_done, n0 + m + 1)
                    act.wait_ge(hid_done, n0 + m + 1)
                    nc.scalar.activation(relu[:, m % BUFS, :], bank[m % BUFS][:], ACT.Relu).then_inc(relu_done, 1)
                    if j == 2 and k < E:
                        act.wait_ge(xsT_done, g * E + (k + 1 + 2))
                        nc.scalar.copy(xs_t[:, (k + 1) % 2, :], bank[4][:]).then_inc(xsT_copied, 1)
                act.wait_ge(out_mm_done, n0 + (NHID + BUFS))
                act.wait_ge(out_rows_done, g + (NG + 1))
                nc.scalar.mul(out_t[:], bank[3][:], 0.5).then_inc(outT_copied, 1)

        def fill(s):
            order = []
            for m in range(NHID + PLAG):
                order += [("hid", m)] * (m < NHID) + [("out", m - PLAG)] * (m >= PLAG)
            return order[len(order) * s // FILL:len(order) * (s + 1) // FILL] if 0 <= s < FILL else []

        def hidden_of(slots):
            return [m for s in slots for kind, m in fill(s) if kind == "hid"]

        def pe_fill(pe, n, slots):
            for s in slots:
                for kind, m in fill(s):
                    k, j = divmod(m, FJ)
                    if kind == "hid":
                        if k and j == 0:
                            pe.wait_ge(p_xsT_copied, n * E + k)
                        pe.wait_ge(p_relu_done, n * NHID + (m + 1))
                        rhs = xs_t[:, k % 2, 0:PCOLS] if k else ln_t[:, bass.ds(n * PCOLS, PCOLS)]
                        nc.tensor.matmul(bank[4 + m % PBANKS][:, 0:PCOLS], fc_sb[:, k, j * P:(j + 1) * P], rhs,
                                         start=True, stop=True).then_inc(p_hid_mm_done, 1)
                        if j == 1 and k < E:
                            pe.wait_ge(p_xs_done, n * E + (k + 1))
                            if k == 0:
                                pe.wait_ge(krows_copied, n + 1)
                            for b in range(PAIR):
                                last = nc.tensor.transpose(bank[7][:, b * P:(b + 1) * P], xs[:, (k + 1) % 2, b, :],
                                                           ident[:])
                            last.then_inc(p_xsT_done, 1)
                    else:
                        if m == 0:
                            pe.wait_ge(p_outT_copied, n + 1)
                        pe.wait_ge(p_hid_done, n * NHID + (m + 1 + PBUFS))
                        nc.tensor.matmul(bank[6][:, 0:PCOLS], proj_sb[:, m, :], hid_p[:, m % PBUFS, :],
                                         start=(m == 0), stop=(m == NHID - 1)).then_inc(p_out_mm_done, 1)

        def act_fill(act, n, slots):
            for m in hidden_of(slots):
                k, j = divmod(m, FJ)
                act.wait_ge(p_hid_mm_done, n * NHID + (m + 1))
                act.wait_ge(p_hid_done, n * NHID + (m + 1))
                nc.scalar.activation(relu_p[:, m % PBUFS, :], bank[4 + m % PBANKS][:, 0:PCOLS],
                                     ACT.Relu).then_inc(p_relu_done, 1)
                if j == 1 and k < E:
                    act.wait_ge(p_xsT_done, n * E + (k + 1 + 2))
                    nc.scalar.copy(xs_t[:, (k + 1) % 2, 0:PCOLS], bank[7][:, 0:PCOLS]).then_inc(p_xsT_copied, 1)

        def dve_fill(dve, n, slots):
            for m in hidden_of(slots):
                dve.wait_ge(p_relu_done, n * NHID + (m + 1 + PBANKS))
                dve.wait_ge(p_out_mm_done, n * NHID + (m + 1))
                nc.vector.tensor_tensor(hid_p[:, m % PBUFS, :], relu_p[:, m % PBUFS, :], relu_p[:, m % PBUFS, :],
                                        ALU.mult).then_inc(p_hid_done, 1)

        def pool_fill(pool, n, k):
            pool.wait_ge(p_xsT_done, n * E + (k + 1))
            nc.gpsimd.tensor_tensor(xs[:, (k + 1) % 2, 0:PAIR], ln[:, bass.ds(n * PAIR, PAIR), :],
                                    root[:, bass.ds(n * PAIR, PAIR), k:k + 1].to_broadcast([P, PAIR, P]),
                                    ALU.mult).then_inc(p_xs_done, 1)

        def act_next(act, n, part):
            cols = bass.ds(n * PCOLS, PCOLS)
            if part == "out":
                act.wait_ge(p_out_mm_done, n * NHID + (NHID + PBUFS))
                nc.scalar.mul(out_t[:, 0:PCOLS], bank[6][:, 0:PCOLS], 0.5).then_inc(p_outT_copied, 1)
            elif part == "ln":
                act.wait_ge(ln1T_done, n + 1)
                nc.scalar.copy(ln_t[:, cols], bank[7][:, 0:PCOLS]).then_inc(ln1T_copied, 1)
            elif part == "k":
                act.wait_ge(kv_mm_done, n + 1)
                nc.scalar.copy(k_new[:], bank[4][:, 0:PCOLS]).then_inc(kcol_done, 1)
            elif part == "k_rows":
                act.wait_ge(kT_done, n + 1)
                nc.scalar.copy(k_rows[:, bass.ds(n * PAIR, PAIR), :].rearrange("p b d -> p (b d)"),
                               bank[7][:, 0:PCOLS]).then_inc(krows_copied, 1)

        def pe_next(pe, n, part):
            if part == "out":
                pe.wait_ge(p_outT_copied, n + 2)
                for b in range(PAIR):
                    last = nc.tensor.transpose(bank[7][:, b * P:(b + 1) * P], out_t[:, b * P:(b + 1) * P], ident[:])
                last.then_inc(p_out_rows_done, 1)
            elif part == "ln":
                pe.wait_ge(ln1_done, n + 1)
                for b in range(PAIR):
                    last = nc.tensor.transpose(bank[7][:, b * P:(b + 1) * P], ln1[:, b, :], ident[:])
                last.then_inc(ln1T_done, 1)
            elif part == "kv":
                pe.wait_ge(ln1T_copied, n + 1)
                for part in range(2):
                    last = nc.tensor.matmul(bank[4 + part][:, 0:PCOLS], wkv_sb[:, part * P:(part + 1) * P],
                                            ln_t[:, bass.ds(n * PCOLS, PCOLS)], start=True, stop=True)
                last.then_inc(kv_mm_done, 1)
            elif part == "kk":
                pe.wait_ge(kcol_done, n + 1)
                for b in range(PAIR):
                    last = nc.tensor.transpose(bank[7][:, b * P:(b + 1) * P], k_new[:, b * P:(b + 1) * P], ident[:])
                last.then_inc(kT_done, 1)
                for b in range(PAIR):
                    last = nc.tensor.matmul(bank[4][:, b * P:(b + 1) * P], k_new[:, b * P:(b + 1) * P],
                                            k_new[:, b * P:(b + 1) * P], start=True, stop=True)
                last.then_inc(kk_mm_done, 1)

        NORM_STEPS = 15

        def dve_next(dve, n, part):
            X, Y, Z = rs_x[:, 0:PAIR], rs_y[:, 0:PAIR], rs_t[:, 0:PAIR]
            at = {"res": 0, "stats": 1, "aggr": 2, "seed": 3, "newton0": 6, "newton1": 9, "newton2": 12}

            def link(ins):
                step[0] += 1
                ins.then_inc(p_norm_step, 1)
                dve.wait_ge(p_norm_step, n * NORM_STEPS + step[0])

            step = [at.get(part, 0)]
            if part == "res":
                dve.wait_ge(p_out_rows_done, n + 1)
                rows = res[:].rearrange("p b d -> p (b d)")[:, bass.ds(n * PCOLS, PCOLS)]
                link(nc.vector.tensor_tensor(rows, rows, bank[7][:, 0:PCOLS], ALU.add))
            elif part == "stats":
                for b in range(PAIR):
                    last = nc.vector.bn_stats(stats[:, b, :], res[:, bass.ds(n * PAIR + b, 1), :]
                                              .rearrange("p a d -> p (a d)"))
                link(last)
            elif part == "aggr":
                for b in range(PAIR):
                    last = nc.vector.bn_aggr(mv[:, b, :], stats[:, b, :])
                link(last)
            elif part == "seed":
                link(nc.vector.tensor_scalar(X, mv[:, 0:PAIR, 1], EPS, None, ALU.add))
                link(nc.vector.tensor_scalar(Z.bitcast(I32), X.bitcast(I32), 1, None, ALU.logical_shift_right))
                link(nc.vector.tensor_scalar(Y.bitcast(I32), Z.bitcast(I32), -1.0, float(0x5F3759DF),
                                             ALU.mult, ALU.add))
            elif part.startswith("newton"):
                link(nc.vector.tensor_tensor(Z, X, Y, ALU.mult))
                link(nc.vector.scalar_tensor_tensor(Z, Z, -0.5, Y, ALU.mult, ALU.mult))
                link(nc.vector.scalar_tensor_tensor(Y, Z, 1.5, Y, ALU.add, ALU.mult))
            elif part == "ln":
                for b in range(PAIR):
                    last = nc.vector.tensor_scalar(ln1[:, b, :], res[:, bass.ds(n * PAIR + b, 1), :]
                                                   .rearrange("p a d -> p (a d)"), mv[:, b, 0:1], rs_y[:, b:b + 1],
                                                   ALU.subtract, ALU.mult)
                last.then_inc(ln1_done, 1)
            elif part == "v":
                dve.wait_ge(kv_mm_done, n + 1)
                nc.vector.tensor_copy(v_t[:, bass.ds(n * PCOLS, PCOLS)], bank[5][:, 0:PCOLS]).then_inc(vcol_done, 1)
            elif part == "k":
                dve.wait_ge(kcol_done, n + 1)
                nc.vector.tensor_copy(k_t[:, bass.ds(n * PCOLS, PCOLS)], k_new[:]).then_inc(kcopy_done, 1)
            elif part == "kk":
                dve.wait_ge(kk_mm_done, n + 1)
                nc.vector.scalar_tensor_tensor(
                    kk[:, bass.ds(n * PAIR, PAIR), :], bank[4][:, 0:PCOLS].rearrange("p (b d) -> p b d", d=P), 1.0,
                    nmask[:].rearrange("p b t -> p (b t)").unsqueeze(1).to_broadcast([P, PAIR, P]),
                    ALU.add, ALU.mult).then_inc(kk_done, 1)

        def mm(out_bank, lhs_t, rhs, start=True, stop=True):
            return nc.tensor.matmul(out_bank[:, 0:P], lhs_t, rhs, start=start, stop=stop)

        mask = nmask[:].rearrange("p b t -> p (b t)")

        block = ctx.enter_context(nc.Block())

        @block.sync
        def _(sp):
            for b in range(B):
                sp.dma_start(res[b * STEPS:(b + 1) * STEPS, :, :],
                             x[b].rearrange("(c t) d -> t c d", t=STEPS)).then_inc(x_in, 16)
            for dst, src in ((router_sb, router), (fc_sb, fc), (proj_sb, proj), (wkv_sb, wkv), (wq_sb, wq)):
                sp.dma_start(dst[:], src).then_inc(weights_in, 16)
            load_params(sp, params_in)
            sp.wait_ge(flag_done, 1)
            ok = sp.value_load(flag[0:1, 0:1], min_val=0, max_val=1)
            with sp.If(ok == 0):
                load_params(sp, params_in)
            sp.wait_ge(res_done, 2 * NG + 1)
            for b in range(B):
                sp.dma_start(out[b].rearrange("(c t) d -> t c d", t=STEPS),
                             res[b * STEPS:(b + 1) * STEPS, :, :]).then_inc(stored, 16)
            sp.wait_ge(stored, 16 * B)

        @block.gpsimd
        def _(pool):
            pool.sem_inc(gap_done, 1)
            nc.gpsimd.memset(ident[:], 0.0)
            nc.gpsimd.memset(nmask[:], -1.0)
            nc.gpsimd.memset(rowmask[:], 0.0)
            nc.gpsimd.memset(gap_sum[:], 0.0)
            nc.gpsimd.memset(ones[:], 1.0).then_inc(consts_made, 1)
            pool.wait_ge(consts_made, 1)
            nc.gpsimd.iota(iota_e[:], pattern=[[0, NBLK], [1, E]], base=0, channel_multiplier=0,
                           allow_small_or_imprecise_dtypes=True)
            nc.gpsimd.affine_select(out=ident[:], in_=ident[:], compare_op=ALU.not_equal, fill=1.0, base=0,
                                    pattern=[[-1, P]], channel_multiplier=1).then_inc(consts_made, 1)
            for b in range(B):
                h = slice(b * STEPS, (b + 1) * STEPS)
                pool.wait_ge(consts_made, 2 + b)
                nc.gpsimd.affine_select(out=nmask[h], in_=nmask[h], compare_op=ALU.is_gt, fill=0.0, base=0,
                                        pattern=[[0, B], [1, STEPS]], channel_multiplier=-1)
                nc.gpsimd.affine_select(out=rowmask[h], in_=rowmask[h], compare_op=ALU.not_equal, fill=1.0,
                                        base=0, pattern=[[-1, STEPS]], channel_multiplier=1)\
                  .then_inc(consts_made, 1)
            pool.wait_ge(consts_made, 2 + B)

            def ffn():
                pool.wait_ge(root_done, 2)
                with pool.Fori(0, NG) as g:
                    for k in range(E):
                        pool.wait_ge(xsT_done, g * E + (k + 1))
                        nc.gpsimd.tensor_tensor(xs[:, (k + 1) % 2], ln[:, bass.ds(g * GRP, GRP), :],
                                                root[:, bass.ds(g * GRP, GRP), k:k + 1].to_broadcast([P, GRP, P]),
                                                ALU.mult).then_inc(xs_done, 1)

            def scan_pair(b, n):
                if n is not None:
                    pool_fill(pool, n, 0)
                    pool_fill(pool, n, 1)
                for q in range(PAIR):
                    c = b * PAIR + q
                    for i in range(ITERS):
                        pool.wait_ge(a_done, c * ITERS + (i + 1))
                        nc.gpsimd.tensor_tensor(slope_u[:], a_t[:], sg[:], ALU.mult)
                        nc.gpsimd.tensor_tensor(slope_v[:], a_t[:], sg[:], ALU.add).then_inc(pool_step, 1)
                        pool.wait_ge(pool_step, c * ITERS + (i + 1))
                        nc.gpsimd.tensor_tensor(slope[:], slope_v[:], slope_u[:],
                                                ALU.subtract).then_inc(slope_done, 1)
                        if n is not None and 2 <= q * ITERS + i + 1 < E:
                            pool_fill(pool, n, q * ITERS + i + 1)
                    new, old = (ITERS - 1) % 2, ITERS % 2
                    pool.wait_ge(esrows_done, (c + 1) * ITERS)
                    pool.wait_ge(d_done, (c + 1) * ITERS)
                    nc.gpsimd.tensor_tensor(gap[:, 3, :], d_rows[:, new, :], d_rows[:, old, :], ALU.subtract)
                    nc.gpsimd.tensor_tensor(gap[:, 2, :], es_rows[:, new, 0, :], es_rows[:, old, 0, :], ALU.subtract)
                    nc.gpsimd.tensor_copy(gap[:, 0, :], es_rows[:, new, 0, :])
                    nc.gpsimd.tensor_copy(gap[:, 1, :], d_rows[:, new, :]).then_inc(gap_done, 1)
                    pool.wait_ge(gap_done, c + 2)
                    nc.gpsimd.tensor_tensor(gap_sq[:], gap[:], gap[:], ALU.mult).then_inc(gap_step, 1)
                    pool.wait_ge(gap_step, 2 * c + 1)
                    nc.gpsimd.tensor_tensor(gap_sum[:], gap_sum[:], gap_sq[:], ALU.add).then_inc(gap_step, 1)
                    pool.wait_ge(gap_step, 2 * c + 2)

            pool.wait_ge(root_done, 1)
            for k in range(E):
                pool_fill(pool, 0, k)
            with pool.Fori(0, NPAIR - 1) as b:
                scan_pair(b, b + 1)
            scan_pair(NPAIR - 1, None)
            ffn()

        @block.scalar
        def _(act):
            act.sem_inc(relu_done, BUFS)
            act.sem_inc(outT_copied, 1)
            act.sem_inc(p_relu_done, PBANKS)
            act.sem_inc(p_outT_copied, 1)
            act.sem_inc(krows_copied, 1)
            act_ffn(act, 0)

            def scan_pair(b, n):
                act.wait_ge(krows_copied, b + 2)
                for q in range(PAIR):
                    c = b * PAIR + q
                    act.wait_ge(upd_done, 5 * c + 1)
                    nc.scalar.copy(krow_now[:], k_rows[:, bass.ds(c, 1), :].rearrange("p a d -> p (a d)"))\
                      .then_inc(know_done, 1)
                    for i in range(ITERS):
                        n1 = c * ITERS + (i + 1)
                        t = q * ITERS + i
                        act.wait_ge(h_done, n1)
                        nc.scalar.activation(sg[:], bank[0][:, 0:P], ACT.Sigmoid, bias=b1_sb[:]).then_inc(sg_done, 1)
                        if n is not None:
                            act_fill(act, n, (5 * t - 1, 5 * t))
                            if t == 10:
                                act_next(act, n, "out")
                            if t == 13:
                                act_next(act, n, "ln")
                        act.wait_ge(aT_done, n1)
                        nc.scalar.copy(a_rows[:], bank[0][:, P:2 * P]).then_inc(arows_done, 1)
                        if n is not None:
                            act_fill(act, n, (5 * t + 1, 5 * t + 2))
                            if t == 13:
                                act_next(act, n, "k")
                        act.wait_ge(esT_done, n1)
                        if i < 2:
                            act.wait_ge(gap_done, c + 1)
                        nc.scalar.copy(es_rows[:, i % 2].rearrange("p a d -> p (a d)"),
                                       bank[0][:, 2 * P:4 * P]).then_inc(esrows_done, 1)
                        if n is not None:
                            act_fill(act, n, (5 * t + 3,))
                if n is not None:
                    act_next(act, n, "k_rows")

            act_fill(act, 0, range(FILL))
            for part in ("out", "ln", "k", "k_rows"):
                act_next(act, 0, part)
            act.wait_ge(krows_copied, 2)
            act.wait_ge(params_in, 16 * 5)
            nc.scalar.activation(unused[:], k_rows[:, 0, 0:1], ACT.Sigmoid)
            with act.Fori(0, NPAIR - 1) as b:
                scan_pair(b, b + 1)
            scan_pair(NPAIR - 1, None)

            act.wait_ge(flag_done, 1)
            ok = act.value_load(flag[0:1, 0:1], min_val=0, max_val=1)
            with act.If(ok == 0):
                act.wait_ge(params_in, 16 * 10)
                with act.Fori(0, NBLK) as c:
                    act.wait_ge(s_upd, c * STEPS + 1)
                    nc.scalar.copy(krow_now[:], k_rows[:, bass.ds(c, 1), :].rearrange("p a d -> p (a d)"))\
                      .then_inc(s_know, 1)
                    with act.Fori(0, STEPS) as t:
                        n1 = c * STEPS + t + 1
                        act.wait_ge(s_h, n1)
                        nc.scalar.activation(sg[:], bank[0][:, 0:P], ACT.Sigmoid, bias=b1_sb[:]).then_inc(s_sg, 1)
                        act.wait_ge(s_aT, n1)
                        nc.scalar.copy(a_rows[:], bank[5][:, 0:P]).then_inc(s_arows, 1)
                        act.wait_ge(s_slopeT, n1)
                        nc.scalar.copy(es_rows[:, 0, 1, :], bank[7][:, 0:P]).then_inc(s_sloperows, 1)
                act.wait_ge(s_params, 5 * S + 1)

            with act.Fori(0, NG) as g:
                act.wait_ge(q_done, g + 1)
                nc.scalar.copy(xs_t[:, 0, :], bank[0][:]).then_inc(q_copied, 1)
                act.wait_ge(qh_done, g + 1)
                nc.scalar.activation(relu[:, 0, :], bank[1][:], ACT.Sigmoid, bias=b1_sb[:]).then_inc(qsg_done, 1)
                act.wait_ge(qy_done, g + 1)
                act.wait_ge(out_rows_done, g + 1)
                nc.scalar.activation(out_t[:], bank[3][:], ACT.Identity, bias=b2_sb[:]).then_inc(outT_copied, 1)
            act_ffn(act, 1)

        @block.vector
        def _(dve):
            at = [0]
            dve.sem_inc(hid_done, BUFS)
            for starts_at_1 in (res_done, params_done, s_params):
                dve.sem_inc(starts_at_1, 1)

            dve.sem_inc(p_hid_done, PBUFS)

            def update(params, signal):
                for w, sums, count in params:
                    dve.wait_ge(upd_done if signal is params_done else s_upd, count)
                    nc.vector.tensor_tensor(w, w, sums, ALU.subtract).then_inc(signal, 1)

            def scan_pair(b, n):
                def side(t, point):
                    if n is None:
                        return
                    dve_fill(dve, n, {"d": (5 * t - 4, 5 * t - 3), "a": (5 * t - 2,),
                                      "ee": (5 * t - 1, 5 * t)}[point])
                    for part in {(10, "ee"): ("res",), (11, "d"): ("stats",), (11, "a"): ("aggr",),
                                 (11, "ee"): ("seed",), (12, "d"): ("newton0",), (12, "a"): ("newton1",),
                                 (12, "ee"): ("newton2", "ln"), (13, "ee"): ("v", "k")}.get((t, point), ()):
                        dve_next(dve, n, part)

                for q in range(PAIR):
                    c = b * PAIR + q
                    dve.wait_ge(params_done, 5 * c + 1)
                    nc.vector.tensor_scalar(v_now[:], v_t[:, col(c)], b2_sb[:], GRAD, ALU.subtract,
                                            ALU.mult).then_inc(vnow_done, 1)
                    dve.wait_ge(vnow_done, c + 1)
                    for i in range(ITERS):
                        n1 = c * ITERS + (i + 1)
                        t = q * ITERS + i
                        side(t, "d")
                        dve.wait_ge(sg_done, n1)
                        silu_rest(a_t[:], bank[0][:, 0:P], b1_sb[:], sg[:]).then_inc(a_done, 1)
                        side(t, "a")
                        dve.wait_ge(y_done, n1)
                        nc.vector.scalar_tensor_tensor(e_t[:], bank[1][:, 0:P], GRAD, v_now[:], ALU.mult,
                                                       ALU.subtract).then_inc(e_done, 1)
                        if i < ITERS - 1:
                            dve.wait_ge(aa_mm_done, c * (ITERS - 1) + (i + 1))
                            nc.vector.scalar_tensor_tensor(aa[:], bank[3][:, 0:P], 1.0, mask, ALU.add,
                                                           ALU.mult).then_inc(aa_done, 1)
                        dve.wait_ge(ee_mm_done, n1)
                        nc.vector.tensor_tensor(ee[:], bank[1][:, 0:P], mask, ALU.mult).then_inc(ee_done, 1)
                        side(t, "ee")
                        dve.wait_ge(da_done, n1)
                        dve.wait_ge(esrows_done, n1)
                        if i < 2:
                            dve.wait_ge(gap_done, c + 1)
                        nc.vector.tensor_tensor(d_rows[:, i % 2, :], bank[2][:, 0:P], es_rows[:, i % 2, 1, :],
                                                ALU.mult).then_inc(d_done, 1)
                    update(((w2_sb[:], bank[3][:, 0:P], 5 * c + 3), (b2_sb[:], bank[3][:, P:P + 1], 5 * c + 3),
                            (w2t_sb[:], bank[1][:, 0:P], 5 * c + 4), (w1_sb[:], bank[0][:, 0:P], 5 * c + 6),
                            (b1_sb[:], bank[0][:, P:P + 1], 5 * c + 6)), params_done)
                if n is not None:
                    dve_next(dve, n, "kk")

            dve.wait_ge(x_in, 16 * B)
            dve.wait_ge(consts_made, 2 + B)
            layernorm(dve, at)
            route(dve, at, 0)
            dve_fill(dve, 0, range(FILL))
            for part in ("res", "stats", "aggr", "seed", "newton0", "newton1", "newton2", "ln", "v", "k", "kk"):
                dve_next(dve, 0, part)
            dve.wait_ge(vcol_done, 1)
            dve.wait_ge(params_in, 16 * 5)
            with dve.Fori(0, NPAIR - 1) as b:
                scan_pair(b, b + 1)
                dve.wait_ge(vcol_done, b + 2)
            scan_pair(NPAIR - 1, None)

            dve.wait_ge(gap_step, 2 * NBLK)
            nc.vector.tensor_reduce(norms[:], gap_sum[:], AX.X, ALU.add).then_inc(norms_done, 1)
            dve.wait_ge(total_done, 1)
            dve_link(dve, nc.vector.tensor_copy(nrm[:], bank[7][0:1, 0:4]), at)
            dve_link(dve, nc.vector.scalar_tensor_tensor(good[:], nrm[:, 0:2], TOL * TOL, nrm[:, 2:4],
                                                         ALU.mult, ALU.is_ge), at)
            dve_link(dve, nc.vector.tensor_tensor(n_good[:], good[:, 0:1], good[:, 1:2], ALU.mult), at)
            dve.wait_ge(params_done, 5 * NBLK + 1)
            nc.vector.tensor_copy(flag[:], n_good[:]).then_inc(flag_done, 1)

            dve.wait_ge(flag_done, 1)
            ok = dve.value_load(flag[0:1, 0:1], min_val=0, max_val=1)
            with dve.If(ok == 0):
                dve.wait_ge(params_in, 16 * 10)
                with dve.Fori(0, NBLK) as c:
                    with dve.Fori(0, STEPS) as t:
                        n = c * STEPS + t
                        own = rowmask[:, bass.ds(t, 1)]
                        dve.wait_ge(s_params, 5 * n + 1)
                        nc.vector.tensor_scalar(v_now[:], v_t[:, col(c)], b2_sb[:], GRAD, ALU.subtract,
                                                ALU.mult).then_inc(s_step, 1)
                        dve.wait_ge(s_step, 3 * n + 1)
                        dve.wait_ge(s_sg, n + 1)
                        silu_rest(a_t[:], bank[0][:, 0:P], b1_sb[:], sg[:]).then_inc(s_a, 1)
                        dve.wait_ge(s_y, n + 1)
                        nc.vector.scalar_tensor_tensor(e_t[:], bank[1][:, 0:P], GRAD, v_now[:], ALU.mult,
                                                       ALU.subtract).then_inc(s_e, 1)
                        dve.wait_ge(s_a, n + 1)
                        nc.vector.scalar_tensor_tensor(slope_u[:], sg[:], 1.0, a_t[:], ALU.subtract,
                                                       ALU.mult).then_inc(s_step, 1)
                        dve.wait_ge(s_step, 3 * n + 2)
                        nc.vector.tensor_tensor(slope[:], sg[:], slope_u[:], ALU.subtract).then_inc(s_slope, 1)
                        dve.wait_ge(s_eT, n + 1)
                        nc.vector.tensor_scalar(es_rows[:, 0, 0, :], bank[6][:, 0:P], own, None,
                                                ALU.mult).then_inc(s_ed, 1)
                        dve.wait_ge(s_da, n + 1)
                        dve.wait_ge(s_sloperows, n + 1)
                        nc.vector.tensor_tensor(d_rows[:, 1, :], bank[2][:, 0:P], es_rows[:, 0, 1, :],
                                                ALU.mult).then_inc(s_step, 1)
                        dve.wait_ge(s_step, 3 * n + 3)
                        nc.vector.tensor_scalar(d_rows[:, 0, :], d_rows[:, 1, :], own, None,
                                                ALU.mult).then_inc(s_ed, 1)
                        update(((w2_sb[:], bank[3][:, 0:P], n + 2), (w2t_sb[:], bank[4][:, 0:P], n + 2),
                                (b2_sb[:], bank[6][:, 0:1], n + 2), (w1_sb[:], bank[0][:, 0:P], n + 2),
                                (b1_sb[:], bank[5][:, 0:1], n + 2)), s_params)
                dve.wait_ge(s_params, 5 * S + 1)

            with dve.Fori(0, NG) as g:
                dve.wait_ge(qsg_done, g + 1)
                silu_rest(hid[:, 0, :], bank[1][:], b1_sb[:], relu[:, 0, :]).then_inc(qa_done, 1)
                add_out_rows(dve, g, g)
            dve.wait_ge(res_done, NG + 1)
            layernorm(dve, at)
            route(dve, at, 1)
            with dve.Fori(0, NG) as g:
                for m in range(NHID):
                    dve.wait_ge(relu_done, g * NHID + (m + 1 + BUFS))
                    dve.wait_ge(out_mm_done, g * NHID + (m + 1))
                    nc.vector.tensor_tensor(hid[:, m % BUFS, :], relu[:, m % BUFS, :], relu[:, m % BUFS, :],
                                            ALU.mult).then_inc(hid_done, 1)
                add_out_rows(dve, g + NG, g)

        @block.tensor
        def _(pe):
            pe.sem_inc(out_mm_done, BUFS)
            pe.sem_inc(xsT_done, 2)
            for starts_at_1 in (out_rows_done, upd_done, s_upd):
                pe.sem_inc(starts_at_1, 1)
            pe.wait_ge(consts_made, 2 + B)
            pe.wait_ge(weights_in, 16 * 5)
            pe.sem_inc(p_out_mm_done, PBUFS)
            pe.sem_inc(p_xsT_done, 2)

            def scan_pair(b, n):
                def side(t, *slots):
                    if n is None:
                        return
                    pe_fill(pe, n, [5 * t + s for s in slots])
                    for part in {(10, 2): ("out",), (13, 0): ("ln",), (13, 2): ("kv",), (13, 4): ("kk",)}\
                            .get((t, slots[0]), ()):
                        pe_next(pe, n, part)

                for q in range(PAIR):
                    c = b * PAIR + q
                    for i in range(ITERS):
                        n1 = c * ITERS + (i + 1)
                        t = q * ITERS + i
                        new, old = i % 2, (i + 1) % 2
                        if i == 0:
                            pe.wait_ge(params_done, 5 * c + 1)
                            mm(bank[0], w1_sb[:], k_t[:, col(c)]).then_inc(h_done, 1)
                        else:
                            pe.wait_ge(esrows_done, c * ITERS + i)
                            mm(bank[0], w1_sb[:], k_t[:, col(c)], stop=False)
                            pe.wait_ge(aa_done, c * (ITERS - 1) + i)
                            mm(bank[1], es_rows[:, old, 0, :], aa[:], stop=False)
                            pe.wait_ge(d_done, c * ITERS + i)
                            mm(bank[0], d_rows[:, old, :], kk[:, bass.ds(c, 1), :].rearrange("p a d -> p (a d)"),
                               start=False).then_inc(h_done, 1)
                        side(t, 0, 1)
                        pe.wait_ge(a_done, n1)
                        mm(bank[1], w2_sb[:], a_t[:], start=(i == 0)).then_inc(y_done, 1)
                        nc.tensor.transpose(bank[0][:, P:2 * P], a_t[:], ident[:]).then_inc(aT_done, 1)
                        if i < ITERS - 1:
                            mm(bank[3], a_t[:], a_t[:]).then_inc(aa_mm_done, 1)
                        side(t, 2)
                        pe.wait_ge(e_done, n1)
                        mm(bank[1], e_t[:], e_t[:]).then_inc(ee_mm_done, 1)
                        mm(bank[2], e_t[:], w2t_sb[:], stop=False)
                        pe.wait_ge(slope_done, n1)
                        pe.wait_ge(arows_done, n1)
                        nc.tensor.transpose(bank[0][:, 2 * P:3 * P], e_t[:], ident[:])
                        nc.tensor.transpose(bank[0][:, 3 * P:4 * P], slope[:], ident[:]).then_inc(esT_done, 1)
                        side(t, 3)
                        pe.wait_ge(ee_done, n1)
                        mm(bank[2], ee[:], a_rows[:], start=False).then_inc(da_done, 1)
                        if i < ITERS - 1:
                            side(t, 4)
                    e_last, d_last = es_rows[:, (ITERS - 1) % 2, 0, :], d_rows[:, (ITERS - 1) % 2, :]
                    pe.wait_ge(esrows_done, (c + 1) * ITERS)
                    mm(bank[3], a_rows[:], e_last).then_inc(upd_done, 1)
                    nc.tensor.matmul(bank[3][:, P:P + 1], e_last, ones[:, 0:1], start=True, stop=True)\
                      .then_inc(upd_done, 1)
                    mm(bank[1], e_last, a_rows[:]).then_inc(upd_done, 1)
                    pe.wait_ge(know_done, c + 1)
                    pe.wait_ge(d_done, (c + 1) * ITERS)
                    mm(bank[0], krow_now[:], d_last).then_inc(upd_done, 1)
                    nc.tensor.matmul(bank[0][:, P:P + 1], d_last, ones[:, 0:1], start=True, stop=True)\
                      .then_inc(upd_done, 1)
                    side(q * ITERS + ITERS - 1, 4)

            pe_route(pe, 0)
            pe_fill(pe, 0, range(FILL))
            for part in ("out", "ln", "kv", "kk"):
                pe_next(pe, 0, part)
            pe.wait_ge(params_in, 16 * 5)
            with pe.Fori(0, NPAIR - 1) as b:
                pe.wait_ge(kcopy_done, b + 1)
                pe.wait_ge(kk_done, b + 1)
                scan_pair(b, b + 1)
            pe.wait_ge(kcopy_done, NPAIR)
            pe.wait_ge(kk_done, NPAIR)
            scan_pair(NPAIR - 1, None)

            pe.wait_ge(norms_done, 1)
            nc.tensor.matmul(bank[7][0:1, 0:4], ones[:, 0:1], norms[:], start=True, stop=True).then_inc(total_done, 1)
            pe.wait_ge(flag_done, 1)
            ok = pe.value_load(flag[0:1, 0:1], min_val=0, max_val=1)
            with pe.If(ok == 0):
                pe.wait_ge(params_in, 16 * 10)
                with pe.Fori(0, NBLK) as c:
                    with pe.Fori(0, STEPS) as t:
                        pe.wait_ge(s_know, c + 1)
                        n = c * STEPS + t
                        pe.wait_ge(s_params, 5 * n + 1)
                        mm(bank[0], w1_sb[:], k_t[:, col(c)]).then_inc(s_h, 1)
                        pe.wait_ge(s_a, n + 1)
                        mm(bank[1], w2_sb[:], a_t[:]).then_inc(s_y, 1)
                        nc.tensor.transpose(bank[5][:, 0:P], a_t[:], ident[:]).then_inc(s_aT, 1)
                        pe.wait_ge(s_e, n + 1)
                        mm(bank[2], e_t[:], w2t_sb[:]).then_inc(s_da, 1)
                        nc.tensor.transpose(bank[6][:, 0:P], e_t[:], ident[:]).then_inc(s_eT, 1)
                        pe.wait_ge(s_slope, n + 1)
                        nc.tensor.transpose(bank[7][:, 0:P], slope[:], ident[:]).then_inc(s_slopeT, 1)
                        pe.wait_ge(s_arows, n + 1)
                        pe.wait_ge(s_ed, 2 * n + 2)
                        mm(bank[3], a_rows[:], es_rows[:, 0, 0, :])
                        mm(bank[4], es_rows[:, 0, 0, :], a_rows[:])
                        nc.tensor.matmul(bank[6][:, 0:1], es_rows[:, 0, 0, :], ones[:, 0:1], start=True, stop=True)
                        mm(bank[0], krow_now[:], d_rows[:, 0, :])
                        nc.tensor.matmul(bank[5][:, 0:1], d_rows[:, 0, :], ones[:, 0:1], start=True,
                                         stop=True).then_inc(s_upd, 1)
                pe.wait_ge(s_params, 5 * S + 1)

            with pe.Fori(0, NG) as g:
                nc.tensor.matmul(bank[0][:], wq_sb[:], ln_t[:, bass.ds(g * COLS, COLS)],
                                 start=True, stop=True).then_inc(q_done, 1)
                pe.wait_ge(q_copied, g + 1)
                nc.tensor.matmul(bank[1][:], w1_sb[:], xs_t[:, 0, :], start=True, stop=True).then_inc(qh_done, 1)
                pe.wait_ge(qa_done, g + 1)
                nc.tensor.matmul(bank[3][:], w2_sb[:], hid[:, 0, :], start=True, stop=True).then_inc(qy_done, 1)
                pe_out_rows(pe, g)
            pe_route(pe, 1)
            pe_ffn(pe)


def kernel(**inputs):
    import numpy as np
    import concourse.bacc as bacc
    from concourse.bass_utils import run_bass_kernel_spmd

    a = {n: np.asarray(v) for n, v in inputs.items()}
    fc = np.concatenate([a["L0_ffn_shared_fc"][None], a["L0_ffn_w_fc"]], 0)
    proj = np.concatenate([a["L0_ffn_shared_proj"][None], a["L0_ffn_w_proj"]], 0)
    arrays = {
        "x": a["L0_attn_x"],
        "wq": a["L0_attn_W_Q"],
        "wkv": a["L0_attn_W_KV"],
        "w1": a["L0_attn_W1"],
        "b1": a["L0_attn_b1"],
        "w2": a["L0_attn_W2"],
        "w2t": a["L0_attn_W2"].T,
        "b2": a["L0_attn_b2"],
        "router": a["L0_ffn_router_w"].T,
        "fc": fc.transpose(2, 0, 1),
        "proj": proj.reshape(E + 1, P, FJ, P).transpose(3, 0, 2, 1).reshape(P, NHID, P),
    }
    arrays = {n: np.ascontiguousarray(v) for n, v in arrays.items()}
    nc = bacc.Bacc("TRN2", target_bir_lowering=False, num_devices=1)
    args = {n: nc.dram_tensor(n, v.shape, mybir.dt.from_np(v.dtype), kind="ExternalInput").ap()
            for n, v in arrays.items()}
    out = nc.dram_tensor("out", (B, S, P), F32, kind="ExternalOutput").ap()
    mk_macaron(nc, out=out, **args)
    r = run_bass_kernel_spmd(nc, [arrays], core_ids=[0])
    return r.results[0]["out"]
```

```python
from contextlib import ExitStack

import concourse.bass as bass
from concourse import mybir

ALU = mybir.AluOpType
ACT = mybir.ActivationFunctionType
AX = mybir.AxisListType
F32 = mybir.dt.float32
F32R = mybir.dt.float32r
I32 = mybir.dt.int32
U32 = mybir.dt.uint32

P = 128
B = 2
S = 1024
T = B * S
STEPS = P // B
NBLK = T // P
GRP = 4
NG = NBLK // GRP
COLS = GRP * P
E = 8
TOPK = 2
FJ = 4
NHID = (E + 1) * FJ
BUFS = 3
PAIR = 2
NPAIR = NBLK // PAIR
PCOLS = PAIR * P
PBUFS = 6
PBANKS = 2
PLAG = 5
ITERS = 7
COARSE = 3
PASSES = PAIR * ITERS
FIRST = 4
FILL = 5 * (PASSES - 4)
TOL = 3e-5
LR = 1e-3
GRAD = LR * 2.0 / (B * P)
EPS = 1e-5


def mk_macaron(nc, x, wq, wkv, w1, b1, w2, w2t, b2, router, experts, out):
    with ExitStack() as ctx:
        def sb(name, shape, dt=F32):
            return ctx.enter_context(nc.sbuf_tensor(name, shape, dt))

        def psum(name):
            return ctx.enter_context(nc.psum_tensor(name, [P, 512], F32))

        def sem(name):
            return ctx.enter_context(nc.semaphore(name))

        bank = [psum(f"bank{i}") for i in range(8)]

        res = sb("res", [P, NBLK, P])
        ln = sb("ln", [P, NBLK, P])
        ln_t = sb("ln_t", [P, T])
        w_hi = sb("w_hi", [P, E + 1, 2, FJ * P], F32R)
        w_lo = sb("w_lo", [P, E + 1, 2, FJ * P], F32R)
        stage = sb("stage", [P, (E + 1) * 2 * FJ * P])
        router_sb = sb("router_sb", [P, E])
        wq_sb = sb("wq_sb", [P, P])
        wkv_sb = sb("wkv_sb", [P, 2 * P])
        w1_sb = sb("w1_sb", [P, P])
        w2_sb = sb("w2_sb", [P, P])
        w2t_sb = sb("w2t_sb", [P, P])
        b1_sb = sb("b1_sb", [P, 1])
        b2_sb = sb("b2_sb", [P, 1])
        ident = sb("ident", [P, P])
        nmask = sb("nmask", [P, B, STEPS])
        rowmask = sb("rowmask", [P, STEPS])
        iota_e = sb("iota_e", [P, NBLK, E])
        ones = sb("ones", [P, 64])
        stats = sb("stats", [P, NBLK, 6])
        mv = sb("mv", [P, NBLK, 2])
        rs_x = sb("rs_x", [P, NBLK * TOPK])
        rs_y = sb("rs_y", [P, NBLK * TOPK])
        rs_t = sb("rs_t", [P, NBLK * TOPK])
        logits = sb("logits", [P, NBLK, E])
        probs = sb("probs", [P, NBLK, E])
        stat1 = sb("stat1", [P, NBLK])
        stat2 = sb("stat2", [P, NBLK])
        top = sb("top", [P, NBLK, 8])
        topi = sb("topi", [P, NBLK, 8], U32)
        topif = sb("topif", [P, NBLK, 8])
        pick = sb("pick", [P, NBLK, E])
        comb = sb("comb", [P, NBLK, E])
        root = sb("root", [P, NBLK, E + 1])
        ln1 = sb("ln1", [P, PAIR, P])
        k_new = sb("k_new", [P, PCOLS])
        xs = sb("xs", [P, 2, GRP, P])
        xs_hi = sb("xs_hi", [P, 3, COLS], F32R)
        xs_lo = sb("xs_lo", [P, 3, COLS], F32R)
        relu = sb("relu", [P, BUFS, COLS])
        sq = sb("sq", [P, BUFS, COLS])
        hid_hi = sb("hid_hi", [P, BUFS, COLS], F32R)
        hid_lo = sb("hid_lo", [P, BUFS, COLS], F32R)
        relu_p, sq_p, hi_p, lo_p = (v[:].rearrange("p b (a n) -> p (b a) n", n=PCOLS)
                                    for v in (relu, sq, hid_hi, hid_lo))
        out_t = sb("out_t", [P, COLS])
        q_hid = [sq[:, 0, :], sq[:, 1, :], sq[:, 2, :], xs[:, 0].rearrange("p b d -> p (b d)")]
        unused = sb("unused", [P, 1])
        k_t, v_t = stage[:, 0:T], stage[:, T:2 * T]
        k_rows = stage[:, 2 * T:3 * T].rearrange("p (b d) -> p b d", d=P)
        kk = stage[:, 3 * T:4 * T].rearrange("p (b d) -> p b d", d=P)
        q_out = stage[:, 4 * T:4 * T + 2 * COLS].rearrange("p (b n) -> p b n", n=COLS)
        krow_now = sb("krow_now", [P, P])
        v_now = sb("v_now", [P, P])
        sg = sb("sg", [P, P])
        a_t = sb("a_t", [P, P])
        a_rows = sb("a_rows", [P, P])
        aa = sb("aa", [P, P])
        e_t = sb("e_t", [P, P])
        a_r, a_rows_r, aa_r, e_r, ee_r = (sb(n, [P, P], F32R) for n in ("a_r", "a_rows_r", "aa_r", "e_r", "ee_r"))
        w1_r, w2_r, w2t_r, k_r, kk_r = (sb(n, [P, P], F32R) for n in ("w1_r", "w2_r", "w2t_r", "k_r", "kk_r"))
        ed_rows_r = sb("ed_rows_r", [P, 2, 2, P], F32R)
        ed_rows = sb("ed_rows", [P, 3, 2, P])
        th = sb("th", [P, P])
        slope_rows = sb("slope_rows", [P, P])
        b1_half = sb("b1_half", [P, 1])
        ee = sb("ee", [P, P])
        slope_u = sb("slope_u", [P, P])
        slope = sb("slope", [P, P])
        gap = sb("gap", [P, 2, P])
        gap_sq = sb("gap_sq", [P, 4, P])
        norms_now = sb("norms_now", [P, 4])
        norms = sb("norms", [P, 4])
        nrm = sb("nrm", [1, 4])
        good = sb("good", [1, 2])
        n_good = sb("n_good", [1, 1])
        flag = sb("flag", [1, 1], I32)

        x_in = sem("x_in")
        weights_in = sem("weights_in")
        consts_made = sem("consts_made")
        dve_step = sem("dve_step")
        ln_done = sem("ln_done")
        lnT_done = sem("lnT_done")
        lnT_copied = sem("lnT_copied")
        logits_done = sem("logits_done")
        shifted_done = sem("shifted_done")
        exp_done = sem("exp_done")
        root_done = sem("root_done")
        xs_done = sem("xs_done")
        xsT_done = sem("xsT_done")
        xsT_hi = sem("xsT_hi")
        xsT_lo = sem("xsT_lo")
        hid_mm_done = sem("hid_mm_done")
        relu_done = sem("relu_done")
        sq_done = sem("sq_done")
        hi_done = sem("hi_done")
        lo_even_done = sem("lo_even_done")
        lo_odd_done = sem("lo_odd_done")
        w_in = [sem(f"w_in{k}") for k in range(E + 1)]
        w_hi_done = sem("w_hi_done")
        w_lo_done = sem("w_lo_done")
        out_mm_done = sem("out_mm_done")
        outT_copied = sem("outT_copied")
        out_rows_done = sem("out_rows_done")
        res_done = sem("res_done")
        p_xs_done = sem("p_xs_done")
        p_xsT_done = sem("p_xsT_done")
        p_xsT_hi = sem("p_xsT_hi")
        p_xsT_lo = sem("p_xsT_lo")
        p_hid_mm_done = sem("p_hid_mm_done")
        p_relu_done = sem("p_relu_done")
        p_sq_done = sem("p_sq_done")
        p_hi_done = sem("p_hi_done")
        p_lo_done = sem("p_lo_done")
        p_out_mm_done = sem("p_out_mm_done")
        p_outT_copied = sem("p_outT_copied")
        p_out_rows_done = sem("p_out_rows_done")
        p_norm_step = sem("p_norm_step")
        ln1_done = sem("ln1_done")
        ln1T_done = sem("ln1T_done")
        ln1T_copied = sem("ln1T_copied")
        kv_mm_done = sem("kv_mm_done")
        kk_mm_done = sem("kk_mm_done")
        kk_done = sem("kk_done")
        krows_copied = sem("krows_copied")
        kcol_done = sem("kcol_done")
        kcopy_done = sem("kcopy_done")
        vcol_done = sem("vcol_done")
        kT_done = sem("kT_done")
        know_done = sem("know_done")
        round_act = sem("round_act")
        round_dve = sem("round_dve")
        vnow_done = sem("vnow_done")
        h_done = sem("h_done")
        a_done = sem("a_done")
        y_done = sem("y_done")
        athT_done = sem("athT_done")
        arows_done = sem("arows_done")
        aa_mm_done = sem("aa_mm_done")
        aa_done = sem("aa_done")
        e_done = sem("e_done")
        ee_mm_done = sem("ee_mm_done")
        ee_done = sem("ee_done")
        th_done = sem("th_done")
        slope_step = sem("slope_step")
        eT_done = sem("eT_done")
        erows_done = sem("erows_done")
        half_done = sem("half_done")
        slope_done = sem("slope_done")
        da_done = sem("da_done")
        d_done = sem("d_done")
        upd_done = sem("upd_done")
        params_done = sem("params_done")
        gap_done = sem("gap_done")
        gap_step = sem("gap_step")
        s_step = sem("s_step")
        s_eT = sem("s_eT")
        qy_done = sem("qy_done")
        total_done = sem("total_done")
        flag_done = sem("flag_done")
        params_in = sem("params_in")
        s_know = sem("s_know")
        s_h = sem("s_h")
        s_sg = sem("s_sg")
        s_a = sem("s_a")
        s_y = sem("s_y")
        s_aT = sem("s_aT")
        s_arows = sem("s_arows")
        s_e = sem("s_e")
        s_da = sem("s_da")
        s_slope = sem("s_slope")
        s_slopeT = sem("s_slopeT")
        s_sloperows = sem("s_sloperows")
        s_ed = sem("s_ed")
        s_upd = sem("s_upd")
        s_params = sem("s_params")
        q_done = sem("q_done")
        q_copied = sem("q_copied")
        qh_done = sem("qh_done")
        qa_done = sem("qa_done")
        stored = sem("stored")

        def dve_link(dve, ins, at):
            at[0] += 1
            ins.then_inc(dve_step, 1)
            dve.wait_ge(dve_step, at[0])

        def silu_rest(dst, pre, bias, gate):
            return nc.vector.scalar_tensor_tensor(dst, pre, bias, gate, ALU.add, ALU.mult)

        def col(block):
            return bass.ds(block * P, P)

        def rsqrt(dve, at, n):
            X, Y, Z = rs_x[:, 0:n], rs_y[:, 0:n], rs_t[:, 0:n]
            dve_link(dve, nc.vector.tensor_scalar(Z.bitcast(I32), X.bitcast(I32), 1, None, ALU.logical_shift_right), at)
            dve_link(dve, nc.vector.tensor_scalar(Y.bitcast(I32), Z.bitcast(I32), -1.0, float(0x5F3759DF),
                                                  ALU.mult, ALU.add), at)
            for _ in range(3):
                dve_link(dve, nc.vector.tensor_tensor(Z, X, Y, ALU.mult), at)
                dve_link(dve, nc.vector.scalar_tensor_tensor(Z, Z, -0.5, Y, ALU.mult, ALU.mult), at)
                dve_link(dve, nc.vector.scalar_tensor_tensor(Y, Z, 1.5, Y, ALU.add, ALU.mult), at)

        def norm_stats(dve, at, g):
            for b in range(g * GRP, (g + 1) * GRP):
                last = nc.vector.bn_stats(stats[:, b, :], res[:, b, :])
            at[0] += 1
            last.then_inc(dve_step, 1)
            return at[0]

        def norm_moments(dve, at, g, stats_there):
            dve.wait_ge(dve_step, stats_there)
            for b in range(g * GRP, (g + 1) * GRP):
                last = nc.vector.bn_aggr(mv[:, b, :], stats[:, b, :])
            at[0] += 1
            last.then_inc(dve_step, 1)

        def normalise(dve, at):
            dve.wait_ge(dve_step, at[0])
            dve_link(dve, nc.vector.tensor_scalar(rs_x[:, 0:NBLK], mv[:, :, 1], EPS, None, ALU.add), at)
            rsqrt(dve, at, NBLK)
            for b in range(NBLK):
                nc.vector.tensor_scalar(ln[:, b, :], res[:, b, :], mv[:, b, 0:1], rs_y[:, b:b + 1],
                                        ALU.subtract, ALU.mult).then_inc(ln_done, 1)

        def route(dve, at, f):
            n3 = [P, NBLK, E]
            dve.wait_ge(logits_done, f + 1)
            dve_link(dve, nc.vector.tensor_copy(logits[:], bank[6][:, 0:NBLK * E]
                                                .rearrange("p (b e) -> p b e", e=E)), at)
            dve_link(dve, nc.vector.tensor_reduce(stat1[:], logits[:], AX.X, ALU.max), at)
            nc.vector.tensor_tensor(logits[:], logits[:], stat1[:].unsqueeze(2).to_broadcast(n3),
                                    ALU.subtract).then_inc(shifted_done, 1)
            dve.wait_ge(exp_done, f + 1)
            dve_link(dve, nc.vector.tensor_reduce(stat1[:], probs[:], AX.X, ALU.add), at)
            dve_link(dve, nc.vector.reciprocal(stat2[:], stat1[:]), at)
            dve_link(dve, nc.vector.tensor_tensor(probs[:], probs[:], stat2[:].unsqueeze(2).to_broadcast(n3),
                                                  ALU.mult), at)
            for b in range(NBLK):
                last = nc.vector.max(top[:, b, :], probs[:, b, :])
            dve_link(dve, last, at)
            for b in range(NBLK):
                last = nc.vector.max_index(topi[:, b, :], top[:, b, :], probs[:, b, :])
            dve_link(dve, last, at)
            dve_link(dve, nc.vector.tensor_copy(topif[:], topi[:]), at)
            dve_link(dve, nc.vector.tensor_tensor(stat1[:], top[:, :, 0], top[:, :, 1], ALU.add), at)
            dve_link(dve, nc.vector.tensor_scalar(stat1[:], stat1[:], 1e-9, None, ALU.max), at)
            dve_link(dve, nc.vector.reciprocal(stat2[:], stat1[:]), at)
            w_top, root_top = (v[:, 0:NBLK * TOPK] for v in (rs_x, rs_t))
            dve_link(dve, nc.vector.tensor_tensor(w_top.rearrange("p (b k) -> p b k", k=TOPK), top[:, :, 0:TOPK],
                                                  stat2[:].unsqueeze(2).to_broadcast([P, NBLK, TOPK]), ALU.mult), at)
            rsqrt(dve, at, NBLK * TOPK)
            dve_link(dve, nc.vector.tensor_tensor(root_top, w_top, rs_y[:, 0:NBLK * TOPK], ALU.mult), at)
            root_top = root_top.rearrange("p (b k) -> p b k", k=TOPK)
            for k, dst in enumerate((comb, pick)):
                last = nc.vector.tensor_tensor(dst[:], iota_e[:], topif[:, :, k:k + 1].to_broadcast(n3), ALU.is_equal)
            dve_link(dve, last, at)
            for k, dst in enumerate((comb, pick)):
                last = nc.vector.tensor_tensor(dst[:], dst[:], root_top[:, :, k:k + 1].to_broadcast(n3), ALU.mult)
            dve_link(dve, last, at)
            nc.vector.tensor_tensor(root[:, :, 1:], comb[:], pick[:], ALU.add).then_inc(root_done, 1)

        def add_out_rows(dve, u, g):
            dve.wait_ge(out_rows_done, u + 2)
            r = res[:].rearrange("p b d -> p (b d)")[:, bass.ds(g * COLS, COLS)]
            return nc.vector.tensor_tensor(r, r, bank[5][:], ALU.add).then_inc(res_done, 1)

        def split_matmul(out_ap, w_h, w_l, x_h, x_l, start, stop):
            nc.tensor.matmul(out_ap, w_h, x_h, start=start, stop=False)
            nc.tensor.matmul(out_ap, w_h, x_l, start=False, stop=False)
            return nc.tensor.matmul(out_ap, w_l, x_h, start=False, stop=stop)

        def weight_parts(m, which):
            k, j = divmod(m, FJ)
            return (w[:, k, which, j * P:(j + 1) * P] for w in (w_hi, w_lo))

        def load_params(eng, done):
            for dst, src in ((w1_sb, w1), (w2_sb, w2), (w2t_sb, w2t), (b1_sb, b1.rearrange("(p a) -> p a", a=1)),
                             (b2_sb, b2.rearrange("(p a) -> p a", a=1))):
                eng.dma_start(dst[:], src).then_inc(done, 16)

        def pe_route(pe, f):
            for g in range(NG + 1):
                if g < NG:
                    n = f * NG + g
                    if n >= 2:
                        pe.wait_ge(lnT_copied, n - 1)
                    pe.wait_ge(ln_done, f * NBLK + (g + 1) * GRP)
                    for b in range(GRP):
                        last = nc.tensor.transpose(bank[g % 2][:, b * P:(b + 1) * P], ln[:, g * GRP + b, :], ident[:])
                    last.then_inc(lnT_done, 1)
                if g:
                    pe.wait_ge(lnT_copied, f * NG + g)
                    for b in range((g - 1) * GRP, g * GRP):
                        last = nc.tensor.matmul(bank[6][:, b * E:(b + 1) * E], ln_t[:, b * P:(b + 1) * P],
                                                router_sb[:], start=True, stop=True)
            last.then_inc(logits_done, 1)

        def ffn_groups(eng, group):
            group(0, True, False)
            with eng.Fori(1, NG - 1) as g:
                group(g, False, False)
            group(NG - 1, False, True)

        def xs_buf(k):
            return {E: 2, E + 1: 0}.get(k, k % 2)

        def pe_ffn_group(pe, g, first, last):
            n0 = g * NHID

            def scaled_transposes(k):
                pe.wait_ge(xs_done, g * (E + 1) + (k + 1))
                for b in range(GRP):
                    last_one = nc.tensor.transpose(bank[4][:, b * P:(b + 1) * P], xs[:, k % 2 if k <= E else 0, b, :],
                                                   ident[:])
                last_one.then_inc(xsT_done, 1)

            def project(m):
                if m == 0:
                    pe.wait_ge(outT_copied, g + (NG + 1))
                pe.wait_ge(hi_done, n0 + (m + 1))
                pe.wait_ge(lo_odd_done if m % 2 else lo_even_done, g * (NHID // 2) + (m // 2 + 1))
                split_matmul(bank[3][:], *weight_parts(m % NHID, 1), hid_hi[:, m % BUFS, :], hid_lo[:, m % BUFS, :],
                             m == 0, m % NHID == NHID - 1).then_inc(out_mm_done, 1)

            if first:
                scaled_transposes(0)
            for m in range(NHID):
                k, j = divmod(m, FJ)
                if j == 0:
                    pe.wait_ge(xsT_lo, g * (E + 1) + (k + 1))
                pe.wait_ge(relu_done, n0 + (m + 1))
                split_matmul(bank[m % BUFS][:], *weight_parts(m, 0), xs_hi[:, xs_buf(k), :], xs_lo[:, xs_buf(k), :],
                             True, True).then_inc(hid_mm_done, 1)
                if m >= BUFS or not first:
                    project(m - BUFS)
                if j == 0 and not (k == E and last):
                    scaled_transposes(k + 1)
                if m == BUFS + 1 and not first:
                    pe_out_rows(pe, g + (NG - 1))
            if last:
                for m in range(NHID - BUFS, NHID):
                    project(m)
                pe_out_rows(pe, g + NG)

        def pe_out_rows(pe, u, cols=out_t[:]):
            pe.wait_ge(outT_copied, u + 2)
            pe.wait_ge(res_done, u + 1)
            for b in range(GRP):
                last = nc.tensor.transpose(bank[5][:, b * P:(b + 1) * P], cols[:, b * P:(b + 1) * P], ident[:])
            last.then_inc(out_rows_done, 1)

        def act_ffn(act, f):
            def split_weights(experts):
                for k in experts:
                    act.wait_ge(w_in[k], 16)
                    nc.scalar.copy(w_hi[:, k].rearrange("p a n -> p (a n)"),
                                   stage[:, k * W:(k + 1) * W]).then_inc(w_hi_done, 1)

            if f == 0:
                split_weights(range(5))
            for g in range(NG):
                n = f * NG + g
                act.wait_ge(lnT_done, n + 1)
                nc.scalar.copy(ln_t[:, g * COLS:(g + 1) * COLS], bank[g % 2][:]).then_inc(lnT_copied, 1)
            if f == 0:
                split_weights(range(5, E + 1))
            act.wait_ge(shifted_done, f + 1)
            nc.scalar.activation(probs[:], logits[:], ACT.Exp).then_inc(exp_done, 1)
            if f == 0:
                return
            ffn_groups(act, lambda g, first, last: act_ffn_group(act, g, first, last))

        def act_ffn_group(act, g, first, last):
            n0 = g * NHID

            def transposed(k):
                act.wait_ge(xsT_done, g * (E + 1) + (k + 1 + 2))
                nc.scalar.copy(xs_hi[:, xs_buf(k), :], bank[4][:]).then_inc(xsT_hi, 1)

            def squared(m):
                act.wait_ge(relu_done, n0 + (m + 1 + BUFS))
                act.wait_ge(out_mm_done, n0 + (m + 1))
                nc.scalar.activation(hid_hi[:, m % BUFS, :], relu[:, m % BUFS, :], ACT.Square).then_inc(hi_done, 1)

            def output(g):
                act.wait_ge(out_mm_done, g * NHID + (NHID + BUFS))
                act.wait_ge(out_rows_done, g + (NG + 1))
                nc.scalar.mul(out_t[:], bank[3][:], 0.5).then_inc(outT_copied, 1)

            if first:
                transposed(0)
            for m in range(NHID):
                k, j = divmod(m, FJ)
                act.wait_ge(hid_mm_done, n0 + (m + 1))
                act.wait_ge(sq_done, n0 + (m + 1))
                if m >= BUFS or not first:
                    act.wait_ge(hi_done, n0 + (m + 1 - BUFS))
                nc.scalar.activation(relu[:, m % BUFS, :], bank[m % BUFS][:], ACT.Relu).then_inc(relu_done, 1)
                if m or not first:
                    squared(m - 1)
                if m == BUFS - 1 and not first:
                    output(g - 1)
                if j == 0 and not (k == E and last):
                    transposed(k + 1)
            if last:
                squared(NHID - 1)
                output(g)

        def fill(s):
            order = []
            for m in range(NHID + PLAG):
                order += [("hid", m)] * (m < NHID) + [("out", m - PLAG)]
            s, slots = s - FIRST, FILL - FIRST
            mine = order[len(order) * s // slots:len(order) * (s + 1) // slots] if 0 <= s < slots else []
            return [(kind, m) for kind, m in mine if m >= 0]

        def hidden_of(slots):
            return [m for s in slots for kind, m in fill(s) if kind == "hid"]

        def pe_fill(pe, n, slots, first=False):
            def scaled_transposes(k):
                pe.wait_ge(p_xs_done, n * (E + 1) + (k + 1))
                for b in range(PAIR):
                    last = nc.tensor.transpose(bank[7][:, b * P:(b + 1) * P], xs[:, k % 2, b, :], ident[:])
                last.then_inc(p_xsT_done, 1)

            for s in slots:
                if s == 0:
                    scaled_transposes(0)
                for kind, m in fill(s):
                    k, j = divmod(m, FJ)
                    if kind == "hid":
                        if j == 0:
                            pe.wait_ge(p_xsT_lo, n * (E + 1) + (k + 1))
                            if first:
                                pe.wait_ge(w_hi_done, k + 1)
                                pe.wait_ge(w_lo_done, k + 1)
                            if m == 0 and not first:
                                pe.wait_ge(kk_done, n)
                        pe.wait_ge(p_relu_done, n * NHID + (m + 1))
                        split_matmul(bank[4 + m % PBANKS][:, 0:PCOLS], *weight_parts(m, 0), xs_hi[:, k % 2, 0:PCOLS],
                                     xs_lo[:, k % 2, 0:PCOLS], True, True).then_inc(p_hid_mm_done, 1)
                        if j == 0 and k < E:
                            scaled_transposes(k + 1)
                    else:
                        if m == 0:
                            pe.wait_ge(p_outT_copied, n + 1)
                            pe.wait_ge(krows_copied, n + 1)
                        pe.wait_ge(p_hi_done, n * NHID + (m + 1))
                        pe.wait_ge(p_lo_done, n * NHID + (m + 1 + PBUFS))
                        split_matmul(bank[6][:, 0:PCOLS], *weight_parts(m, 1), hi_p[:, m % PBUFS, :],
                                     lo_p[:, m % PBUFS, :], m == 0, m == NHID - 1).then_inc(p_out_mm_done, 1)

        def act_fill(act, n, slots):
            def transposed(k):
                act.wait_ge(p_xsT_done, n * (E + 1) + (k + 1 + 2))
                nc.scalar.copy(xs_hi[:, k % 2, 0:PCOLS], bank[7][:, 0:PCOLS]).then_inc(p_xsT_hi, 1)

            def squared(m):
                act.wait_ge(p_relu_done, n * NHID + (m + 1 + PBANKS))
                act.wait_ge(p_out_mm_done, n * NHID + (m + 1))
                nc.scalar.activation(hi_p[:, m % PBUFS, :], relu_p[:, m % PBUFS, :],
                                     ACT.Square).then_inc(p_hi_done, 1)

            if 0 in slots:
                transposed(0)
            for m in hidden_of(slots):
                k, j = divmod(m, FJ)
                act.wait_ge(p_hid_mm_done, n * NHID + (m + 1))
                act.wait_ge(p_sq_done, n * NHID + (m + 1))
                nc.scalar.activation(relu_p[:, m % PBUFS, :], bank[4 + m % PBANKS][:, 0:PCOLS],
                                     ACT.Relu).then_inc(p_relu_done, 1)
                if m:
                    squared(m - 1)
                if m == NHID - 1:
                    squared(m)
                if j == 0 and k < E:
                    transposed(k + 1)

        def dve_fill(dve, n, slots):
            def rest_of_transposed(k):
                dve.wait_ge(p_xsT_hi, n * (E + 1) + (k + 1))
                nc.vector.tensor_tensor(xs_lo[:, k % 2, 0:PCOLS], bank[7][:, 0:PCOLS],
                                        xs_hi[:, k % 2, 0:PCOLS].bitcast(F32), ALU.subtract).then_inc(p_xsT_lo, 1)

            if 0 in slots:
                rest_of_transposed(0)
            for m in hidden_of(slots):
                k, j = divmod(m, FJ)
                dve.wait_ge(p_relu_done, n * NHID + (m + 1 + PBANKS))
                dve.wait_ge(p_lo_done, n * NHID + (m + 1))
                nc.vector.tensor_tensor(sq_p[:, m % PBUFS, :], relu_p[:, m % PBUFS, :], relu_p[:, m % PBUFS, :],
                                        ALU.mult).then_inc(p_sq_done, 1)
                if j == 0 and k < E:
                    rest_of_transposed(k + 1)

        def pool_pair(pool, n):
            def scale(k):
                pool.wait_ge(p_xsT_done, n * (E + 1) + (k + 1 + (k == 0)))
                nc.gpsimd.tensor_tensor(xs[:, k % 2, 0:PAIR], ln[:, bass.ds(n * PAIR, PAIR), :],
                                        root[:, bass.ds(n * PAIR, PAIR), k:k + 1].to_broadcast([P, PAIR, P]),
                                        ALU.mult).then_inc(p_xs_done, 1)

            for k in range(3):
                scale(k)
            for m in range(NHID):
                k, j = divmod(m + 1, FJ)
                if m == 0:
                    scale(3)
                elif j == 0 and k + 3 <= E:
                    scale(k + 3)
                pool.wait_ge(p_sq_done, n * NHID + (m + 1 + PBUFS))
                pool.wait_ge(p_hi_done, n * NHID + (m + 1))
                pool.wait_ge(p_out_mm_done, n * NHID + (m + 1))
                nc.gpsimd.tensor_tensor(lo_p[:, m % PBUFS, :], sq_p[:, m % PBUFS, :],
                                        hi_p[:, m % PBUFS, :].bitcast(F32), ALU.subtract).then_inc(p_lo_done, 1)

        def act_next(act, n, part):
            cols = bass.ds(n * PCOLS, PCOLS)
            if part == "out":
                act.wait_ge(p_out_mm_done, n * NHID + (NHID + PBUFS))
                nc.scalar.mul(out_t[:, 0:PCOLS], bank[6][:, 0:PCOLS], 0.5).then_inc(p_outT_copied, 1)
            elif part == "ln":
                act.wait_ge(ln1T_done, n + 1)
                nc.scalar.copy(ln_t[:, cols], bank[7][:, 0:PCOLS]).then_inc(ln1T_copied, 1)
            elif part == "k":
                act.wait_ge(kv_mm_done, 2 * n + 1)
                nc.scalar.copy(k_new[:], bank[4][:, 0:PCOLS]).then_inc(kcol_done, 1)
            elif part == "k_rows":
                nc.scalar.copy(k_rows[:, bass.ds(n * PAIR, PAIR), :].rearrange("p b d -> p (b d)"),
                               bank[6][:, 0:PCOLS]).then_inc(krows_copied, 1)

        def pe_next(pe, n, part):
            if part == "out":
                pe.wait_ge(p_outT_copied, n + 2)
                for b in range(PAIR):
                    last = nc.tensor.transpose(bank[7][:, b * P:(b + 1) * P], out_t[:, b * P:(b + 1) * P], ident[:])
                last.then_inc(p_out_rows_done, 1)
            elif part == "ln":
                pe.wait_ge(ln1_done, n + 1)
                for b in range(PAIR):
                    last = nc.tensor.transpose(bank[7][:, b * P:(b + 1) * P], ln1[:, b, :], ident[:])
                last.then_inc(ln1T_done, 1)
            elif part in ("k", "v"):
                pe.wait_ge(ln1T_copied, n + 1)
                which = "kv".index(part)
                nc.tensor.matmul(bank[4 + which][:, 0:PCOLS], wkv_sb[:, which * P:(which + 1) * P],
                                 ln_t[:, bass.ds(n * PCOLS, PCOLS)], start=True, stop=True).then_inc(kv_mm_done, 1)
            elif part == "kk":
                pe.wait_ge(p_outT_copied, n + 2)
                pe.wait_ge(kcol_done, n + 1)
                for b in range(PAIR):
                    last = nc.tensor.transpose(bank[6][:, b * P:(b + 1) * P], k_new[:, b * P:(b + 1) * P], ident[:])
                last.then_inc(kT_done, 1)
                for b in range(PAIR):
                    last = nc.tensor.matmul(bank[4][:, b * P:(b + 1) * P], k_new[:, b * P:(b + 1) * P],
                                            k_new[:, b * P:(b + 1) * P], start=True, stop=True)
                last.then_inc(kk_mm_done, 1)

        NORM_STEPS = 15
        PARAMS_AHEAD = 4

        def dve_next(dve, n, part):
            X, Y, Z = rs_x[:, 0:PAIR], rs_y[:, 0:PAIR], rs_t[:, 0:PAIR]
            at = {"res": 0, "stats": 1, "aggr": 2, "seed": 3, "newton0": 6, "newton1": 9, "newton2": 12}

            def link(ins):
                step[0] += 1
                ins.then_inc(p_norm_step, 1)
                dve.wait_ge(p_norm_step, n * NORM_STEPS + step[0])

            step = [at.get(part, 0)]
            if part == "res":
                dve.wait_ge(p_out_rows_done, n + 1)
                rows = res[:].rearrange("p b d -> p (b d)")[:, bass.ds(n * PCOLS, PCOLS)]
                link(nc.vector.tensor_tensor(rows, rows, bank[7][:, 0:PCOLS], ALU.add))
            elif part == "stats":
                for b in range(PAIR):
                    last = nc.vector.bn_stats(stats[:, b, :], res[:, bass.ds(n * PAIR + b, 1), :]
                                              .rearrange("p a d -> p (a d)"))
                link(last)
            elif part == "aggr":
                for b in range(PAIR):
                    last = nc.vector.bn_aggr(mv[:, b, :], stats[:, b, :])
                link(last)
            elif part == "seed":
                link(nc.vector.tensor_scalar(X, mv[:, 0:PAIR, 1], EPS, None, ALU.add))
                link(nc.vector.tensor_scalar(Z.bitcast(I32), X.bitcast(I32), 1, None, ALU.logical_shift_right))
                link(nc.vector.tensor_scalar(Y.bitcast(I32), Z.bitcast(I32), -1.0, float(0x5F3759DF),
                                             ALU.mult, ALU.add))
            elif part.startswith("newton"):
                link(nc.vector.tensor_tensor(Z, X, Y, ALU.mult))
                link(nc.vector.scalar_tensor_tensor(Z, Z, -0.5, Y, ALU.mult, ALU.mult))
                link(nc.vector.scalar_tensor_tensor(Y, Z, 1.5, Y, ALU.add, ALU.mult))
            elif part == "ln":
                for b in range(PAIR):
                    last = nc.vector.tensor_scalar(ln1[:, b, :], res[:, bass.ds(n * PAIR + b, 1), :]
                                                   .rearrange("p a d -> p (a d)"), mv[:, b, 0:1], rs_y[:, b:b + 1],
                                                   ALU.subtract, ALU.mult)
                last.then_inc(ln1_done, 1)
            elif part == "v":
                dve.wait_ge(kv_mm_done, 2 * n + 2)
                nc.vector.tensor_copy(v_t[:, bass.ds(n * PCOLS, PCOLS)], bank[5][:, 0:PCOLS]).then_inc(vcol_done, 1)
            elif part == "k":
                dve.wait_ge(kcol_done, n + 1)
                nc.vector.tensor_copy(k_t[:, bass.ds(n * PCOLS, PCOLS)], k_new[:]).then_inc(kcopy_done, 1)
            elif part == "kk":
                dve.wait_ge(kk_mm_done, n + 1)
                nc.vector.scalar_tensor_tensor(
                    kk[:, bass.ds(n * PAIR, PAIR), :], bank[4][:, 0:PCOLS].rearrange("p (b d) -> p b d", d=P), 1.0,
                    nmask[:].rearrange("p b t -> p (b t)").unsqueeze(1).to_broadcast([P, PAIR, P]),
                    ALU.add, ALU.mult).then_inc(kk_done, 1)

        QY_BANK = (4, 6, 7, 0)

        def coarse(i):
            return 1 <= i <= COARSE

        def kind(full, rounded, i):
            return rounded if coarse(i) else full

        def buf(i):
            return 2 if i == ITERS - 1 else i % 2

        def mm(out_bank, lhs_t, rhs, start=True, stop=True):
            return nc.tensor.matmul(out_bank[:, 0:P], lhs_t, rhs, start=start, stop=stop)

        mask = nmask[:].rearrange("p b t -> p (b t)")
        W = 2 * FJ * P

        block = ctx.enter_context(nc.Block())

        @block.sync
        def _(sp):
            for b in range(B):
                sp.dma_start(res[b * STEPS:(b + 1) * STEPS, :, :],
                             x[b].rearrange("(c t) d -> t c d", t=STEPS)).then_inc(x_in, 16)
            sp.dma_start(router_sb[:], router).then_inc(weights_in, 16)
            for k in range(E + 1):
                sp.dma_start(stage[:, k * W:(k + 1) * W], experts[:, k]).then_inc(w_in[k], 16)
            for dst, src in ((wkv_sb, wkv), (wq_sb, wq)):
                sp.dma_start(dst[:], src).then_inc(params_in, 16)
            load_params(sp, params_in)
            sp.wait_ge(flag_done, 1)
            ok = sp.value_load(flag[0:1, 0:1], min_val=0, max_val=1)
            with sp.If(ok == 0):
                load_params(sp, params_in)
            for g in range(NG):
                sp.wait_ge(res_done, NG + g + 2)
                for b in range(B):
                    sp.dma_start(out[b].rearrange("(c t) d -> t c d", t=STEPS)[:, g * GRP:(g + 1) * GRP, :],
                                 res[b * STEPS:(b + 1) * STEPS, g * GRP:(g + 1) * GRP, :]).then_inc(stored, 16)
            sp.wait_ge(stored, 16 * B * NG)

        @block.gpsimd
        def _(pool):
            nc.gpsimd.memset(ident[:], 0.0)
            nc.gpsimd.memset(nmask[:], -1.0)
            nc.gpsimd.memset(rowmask[:], 0.0)
            nc.gpsimd.memset(norms[:], 0.0)
            nc.gpsimd.memset(root[:], 1.0)
            nc.gpsimd.memset(ed_rows[:], 0.0)
            pool.sem_inc(p_lo_done, PBUFS)
            nc.gpsimd.memset(ones[:], 1.0).then_inc(consts_made, 1)
            pool.wait_ge(consts_made, 1)
            nc.gpsimd.iota(iota_e[:], pattern=[[0, NBLK], [1, E]], base=0, channel_multiplier=0,
                           allow_small_or_imprecise_dtypes=True)
            nc.gpsimd.affine_select(out=ident[:], in_=ident[:], compare_op=ALU.not_equal, fill=1.0, base=0,
                                    pattern=[[-1, P]], channel_multiplier=1).then_inc(consts_made, 1)
            for b in range(B):
                h = slice(b * STEPS, (b + 1) * STEPS)
                pool.wait_ge(consts_made, 2 + b)
                nc.gpsimd.affine_select(out=nmask[h], in_=nmask[h], compare_op=ALU.is_gt, fill=0.0, base=0,
                                        pattern=[[0, B], [1, STEPS]], channel_multiplier=-1)
                nc.gpsimd.affine_select(out=rowmask[h], in_=rowmask[h], compare_op=ALU.not_equal, fill=1.0,
                                        base=0, pattern=[[-1, STEPS]], channel_multiplier=1)\
                  .then_inc(consts_made, 1)
            pool.wait_ge(consts_made, 2 + B)

            for k in range(E + 1):
                pool.wait_ge(w_hi_done, k + 1)
                nc.gpsimd.tensor_tensor(w_lo[:, k].rearrange("p a n -> p (a n)"), stage[:, k * W:(k + 1) * W],
                                        w_hi[:, k].rearrange("p a n -> p (a n)").bitcast(F32),
                                        ALU.subtract).then_inc(w_lo_done, 1)
            pool.wait_ge(root_done, 1)
            with pool.Fori(0, NPAIR) as n:
                pool_pair(pool, n)

            pool.wait_ge(root_done, 2)
            def ffn_group(g, first, last):
                def scale(k, g):
                    pool.wait_ge(xsT_done, g * (E + 1) + (k + 1 + (k == 0)))
                    nc.gpsimd.tensor_tensor(xs[:, k % 2], ln[:, bass.ds(g * GRP, GRP), :],
                                            root[:, bass.ds(g * GRP, GRP), k:k + 1].to_broadcast([P, GRP, P]),
                                            ALU.mult).then_inc(xs_done, 1)

                if first:
                    for k in range(3):
                        scale(k, g)
                for m in range(1, NHID, 2):
                    pool.wait_ge(sq_done, g * NHID + (m + 1 + BUFS))
                    pool.wait_ge(hi_done, g * NHID + (m + 1))
                    pool.wait_ge(out_mm_done, g * NHID + (m + 1))
                    nc.gpsimd.tensor_tensor(hid_lo[:, m % BUFS, :], sq[:, m % BUFS, :],
                                            hid_hi[:, m % BUFS, :].bitcast(F32),
                                            ALU.subtract).then_inc(lo_odd_done, 1)
                    k, j = divmod(m + 9, FJ)
                    if j == 0 and k <= E:
                        scale(k, g)
                    elif j == 0 and not last:
                        scale(k - E - 1, g + 1)

            ffn_groups(pool, ffn_group)

        @block.scalar
        def _(act):
            act.sem_inc(relu_done, BUFS)
            act.sem_inc(outT_copied, 1)
            act.sem_inc(p_relu_done, PBANKS)
            act.sem_inc(p_outT_copied, 1)
            act.sem_inc(krows_copied, 1)
            act_ffn(act, 0)

            def scan_pair(b, n):
                def side(t, point):
                    if n is None:
                        u = t - 2
                        if point == "e" and u in range(T // PCOLS):
                            act.wait_ge(q_done, u + 1)
                            nc.scalar.copy(ln_t[:, u * PCOLS:(u + 1) * PCOLS],
                                           bank[4 + u % 2][:, 0:PCOLS]).then_inc(q_copied, 1)
                        return
                    act_fill(act, n, {"a": (), "rows": (5 * t - 1, 5 * t), "slope": (5 * t + 1,),
                                      "e": (5 * t + 2, 5 * t + 3)}[point])
                    for part in {(PASSES - 4, "a"): ("out",), (PASSES - 1, "rows"): ("ln",),
                                 (PASSES - 1, "e"): ("k",)}.get((t, point), ()):
                        act_next(act, n, part)

                for q in range(PAIR):
                    c = b * PAIR + q
                    for i in range(ITERS):
                        n1 = c * ITERS + (i + 1)
                        t = q * ITERS + i
                        act.wait_ge(h_done, n1)
                        nc.scalar.activation(kind(a_t, a_r, i)[:], bank[0][:, 0:P], ACT.Silu,
                                             bias=b1_sb[:]).then_inc(a_done, 1)
                        if i == 0:
                            act.wait_ge(half_done, c + 1)
                        nc.scalar.activation(th[:], bank[0][:, 0:P], ACT.Tanh, bias=b1_half[:],
                                             scale=0.5).then_inc(th_done, 1)
                        side(t, "a")
                        if t == 0:
                            act.wait_ge(kT_done, b + 1)
                        act.wait_ge(athT_done, n1)
                        nc.scalar.copy(kind(a_rows, a_rows_r, i)[:], bank[3][:, 0:P]).then_inc(arows_done, 1)
                        side(t, "rows")
                        if t == 0:
                            act_next(act, b, "k_rows")
                        side(t, "slope")
                        if i == 0:
                            act.wait_ge(krows_copied, b + 2)
                            act.wait_ge(upd_done, 5 * c + 1)
                        act.wait_ge(eT_done, n1)
                        if i in (1, ITERS - 1):
                            act.wait_ge(gap_step, 2 * c + 1 + (i > 1))
                        nc.scalar.copy(kind(ed_rows, ed_rows_r, i + 1)[:, buf(i), 0, :],
                                       bank[3][:, 2 * P:3 * P]).then_inc(erows_done, 1)
                        if i == 0:
                            nc.scalar.copy(krow_now[:], k_rows[:, bass.ds(c, 1), :].rearrange("p a d -> p (a d)"))\
                              .then_inc(know_done, 1)
                            nc.scalar.copy(w1_r[:], w1_sb[:]).then_inc(round_act, 1)
                            nc.scalar.copy(k_r[:], k_t[:, col(c)]).then_inc(round_act, 1)
                        side(t, "e")

            act_fill(act, 0, range(FILL))
            for part in ("out", "ln", "k"):
                act_next(act, 0, part)
            act.wait_ge(params_in, 16 * 7)
            act.wait_ge(kcol_done, 1)
            nc.scalar.activation(unused[:], k_new[:, 0:1], ACT.Silu)
            with act.Fori(0, NPAIR - 1) as b:
                scan_pair(b, b + 1)
            scan_pair(NPAIR - 1, None)

            act.wait_ge(flag_done, 1)
            ok = act.value_load(flag[0:1, 0:1], min_val=0, max_val=1)
            with act.If(ok == 0):
                act.wait_ge(params_in, 16 * 12)
                with act.Fori(0, NBLK) as c:
                    act.wait_ge(s_upd, c * STEPS + 1)
                    nc.scalar.copy(krow_now[:], k_rows[:, bass.ds(c, 1), :].rearrange("p a d -> p (a d)"))\
                      .then_inc(s_know, 1)
                    with act.Fori(0, STEPS) as t:
                        n1 = c * STEPS + t + 1
                        act.wait_ge(s_h, n1)
                        nc.scalar.activation(sg[:], bank[0][:, 0:P], ACT.Sigmoid, bias=b1_sb[:]).then_inc(s_sg, 1)
                        act.wait_ge(s_aT, n1)
                        nc.scalar.copy(a_rows[:], bank[5][:, 0:P]).then_inc(s_arows, 1)
                        act.wait_ge(s_slopeT, n1)
                        nc.scalar.copy(slope_rows[:], bank[7][:, 0:P]).then_inc(s_sloperows, 1)
                act.wait_ge(s_params, 5 * S + 1)

            for g in range(NG):
                act.wait_ge(qh_done, g + 1)
                nc.scalar.activation(q_hid[g], bank[g][:], ACT.Silu, bias=b1_sb[:]).then_inc(qa_done, 1)
            for g in range(NG):
                act.wait_ge(qy_done, g + 1)
                if g >= 2:
                    act.wait_ge(out_rows_done, g)
                nc.scalar.activation(q_out[:, g % 2, :], bank[QY_BANK[g]][:], ACT.Identity,
                                     bias=b2_sb[:]).then_inc(outT_copied, 1)
            act_ffn(act, 1)

        @block.vector
        def _(dve):
            at = [0]
            dve.sem_inc(sq_done, BUFS)
            dve.sem_inc(p_sq_done, PBUFS)
            for starts_at_1 in (res_done, s_params):
                dve.sem_inc(starts_at_1, 1)
            dve.sem_inc(params_done, PARAMS_AHEAD)

            def update(params, signal):
                for w, sums, count in params:
                    dve.wait_ge(upd_done if signal is params_done else s_upd, count)
                    nc.vector.tensor_tensor(w, w, sums, ALU.subtract).then_inc(signal, 1)

            def half_bias(c):
                dve.wait_ge(params_done, 5 * c + 1)
                nc.vector.tensor_scalar(b1_half[:], b1_sb[:], 0.5, None, ALU.mult).then_inc(half_done, 1)

            def targets(c):
                dve.wait_ge(params_done, 5 * c + 3)
                nc.vector.tensor_scalar(v_now[:], v_t[:, col(c)], b2_sb[:], GRAD, ALU.subtract,
                                        ALU.mult).then_inc(vnow_done, 1)

            def compare(u, parts):
                new, old = ed_rows[:, buf(ITERS - 1)], ed_rows[:, buf(ITERS - 2)]
                for part in parts:
                    if part == 0:
                        nc.vector.tensor_tensor(gap[:], new, old, ALU.subtract).then_inc(gap_step, 1)
                    elif part < 5:
                        k = part - 1
                        x = (new[:, 0], new[:, 1], gap[:, 0, :], gap[:, 1, :])[k]
                        dve.wait_ge(gap_step, 2 * u + 1)
                        ins = nc.vector.tensor_tensor_reduce(gap_sq[:, k, :], x, x, 1.0, 0.0, ALU.mult, ALU.add,
                                                             norms_now[:, k:k + 1])
                        if part == 4:
                            ins.then_inc(gap_step, 1)
                    elif part == 5:
                        dve.wait_ge(gap_step, 2 * u + 2)
                        nc.vector.tensor_tensor(norms[:], norms[:], norms_now[:], ALU.add).then_inc(gap_done, 1)

            def scan_pair(b, n):
                def side(t, point):
                    if n is None:
                        return
                    dve_fill(dve, n, {"start": (5 * t - 2,), "d": (5 * t - 1, 5 * t),
                                      "ee": (5 * t + 1, 5 * t + 2)}[point])
                    for part in {(PASSES - 4, "ee"): ("res",), (PASSES - 3, "start"): ("stats",),
                                 (PASSES - 3, "d"): ("aggr",), (PASSES - 3, "ee"): ("seed", "newton0"),
                                 (PASSES - 2, "d"): ("newton1",),
                                 (PASSES - 2, "ee"): ("newton2", "ln")}.get((t, point), ()):
                        dve_next(dve, n, part)

                for q in range(PAIR):
                    c = b * PAIR + q
                    for i in range(ITERS):
                        n1 = c * ITERS + (i + 1)
                        t = q * ITERS + i
                        side(t, "start")
                        if i == 0:
                            dve.wait_ge(vnow_done, c + 1)
                        dve.wait_ge(y_done, n1)
                        nc.vector.scalar_tensor_tensor(kind(e_t, e_r, i)[:], bank[1][:, 0:P], GRAD, v_now[:], ALU.mult,
                                                       ALU.subtract).then_inc(e_done, 1)
                        if i < ITERS - 1:
                            dve.wait_ge(aa_mm_done, c * (ITERS - 1) + (i + 1))
                            nc.vector.scalar_tensor_tensor(kind(aa, aa_r, i + 1)[:], bank[0][:, 0:P], 1.0, mask,
                                                           ALU.add, ALU.mult).then_inc(aa_done, 1)
                        dve.wait_ge(arows_done, n1)
                        rows_now = kind(a_rows, a_rows_r, i)[:].bitcast(F32)
                        nc.vector.scalar_tensor_tensor(slope_u[:], rows_now, 1.0, bank[3][:, P:2 * P], ALU.subtract,
                                                       ALU.mult).then_inc(slope_step, 1)
                        dve.wait_ge(slope_step, n1)
                        nc.vector.scalar_tensor_tensor(slope_rows[:], slope_u[:], 1.0, rows_now, ALU.subtract,
                                                       ALU.subtract).then_inc(slope_done, 1)
                        if t == 0:
                            dve_next(dve, b, "kk")
                        side(t, "d")
                        dve.wait_ge(da_done, n1)
                        dve.wait_ge(slope_done, n1)
                        if i in (1, ITERS - 1):
                            dve.wait_ge(gap_step, 2 * c + 1 + (i > 1))
                        nc.vector.scalar_tensor_tensor(kind(ed_rows, ed_rows_r, i + 1)[:, buf(i), 1, :],
                                                       bank[2][:, 0:P], -0.5, slope_rows[:], ALU.mult,
                                                       ALU.mult).then_inc(d_done, 1)
                        if i < ITERS - 1:
                            if t == 0:
                                dve.wait_ge(kk_done, b + 1)
                            dve.wait_ge(ee_mm_done, c * (ITERS - 1) + (i + 1))
                            nc.vector.tensor_tensor(kind(ee, ee_r, i + 1)[:], bank[1][:, 0:P], mask,
                                                    ALU.mult).then_inc(ee_done, 1)
                        if i == 0:
                            nc.vector.tensor_copy(kk_r[:], kk[:, bass.ds(c, 1), :].rearrange("p a d -> p (a d)"))\
                              .then_inc(round_dve, 1)
                            dve.wait_ge(params_done, 5 * c + 4)
                            nc.vector.tensor_copy(w2_r[:], w2_sb[:]).then_inc(round_dve, 1)
                            nc.vector.tensor_copy(w2t_r[:], w2t_sb[:]).then_inc(round_dve, 1)
                        if i < 6:
                            compare(c, (i,))
                        side(t, "ee")
                    more = n is not None or q < PAIR - 1
                    update(((w1_sb[:], bank[0][:, 0:P], 5 * c + 3), (b1_sb[:], bank[0][:, P:P + 1], 5 * c + 3),
                            (w2_sb[:], bank[3][:, 0:P], 5 * c + 5), (b2_sb[:], bank[3][:, P:P + 1], 5 * c + 5)),
                           params_done)
                    if more:
                        half_bias(c + 1)
                    if n is not None and q == PAIR - 1:
                        dve_next(dve, n, "k")
                    update(((w2t_sb[:], bank[1][:, 0:P], 5 * c + 6),), params_done)
                    if more:
                        if q == PAIR - 1:
                            dve_next(dve, n, "v")
                            dve.wait_ge(vcol_done, n + 1)
                        targets(c + 1)

            dve.wait_ge(x_in, 16 * B)
            dve.wait_ge(consts_made, 2 + B)
            for g in range(NG):
                stats_there = norm_stats(dve, at, g)
            for g in range(NG):
                norm_moments(dve, at, g, stats_there)
            normalise(dve, at)
            route(dve, at, 0)
            dve_fill(dve, 0, range(FILL))
            for part in ("res", "stats", "aggr", "seed", "newton0", "newton1", "newton2", "ln", "v", "k"):
                dve_next(dve, 0, part)
            dve.wait_ge(vcol_done, 1)
            dve.wait_ge(params_in, 16 * 7)
            half_bias(0)
            targets(0)
            with dve.Fori(0, NPAIR - 1) as b:
                scan_pair(b, b + 1)
            scan_pair(NPAIR - 1, None)
            compare(NBLK, range(6))

            dve.wait_ge(total_done, 1)
            dve_link(dve, nc.vector.tensor_copy(nrm[:], bank[7][0:1, 0:4]), at)
            dve_link(dve, nc.vector.scalar_tensor_tensor(good[:], nrm[:, 0:2], TOL * TOL, nrm[:, 2:4],
                                                         ALU.mult, ALU.is_ge), at)
            dve_link(dve, nc.vector.tensor_tensor(n_good[:], good[:, 0:1], good[:, 1:2], ALU.mult), at)
            dve.wait_ge(params_done, 5 * NBLK + PARAMS_AHEAD)
            nc.vector.tensor_copy(flag[:], n_good[:]).then_inc(flag_done, 1)

            dve.wait_ge(flag_done, 1)
            ok = dve.value_load(flag[0:1, 0:1], min_val=0, max_val=1)
            with dve.If(ok == 0):
                dve.wait_ge(params_in, 16 * 12)
                with dve.Fori(0, NBLK) as c:
                    with dve.Fori(0, STEPS) as t:
                        n = c * STEPS + t
                        own = rowmask[:, bass.ds(t, 1)]
                        dve.wait_ge(s_params, 5 * n + 1)
                        nc.vector.tensor_scalar(v_now[:], v_t[:, col(c)], b2_sb[:], GRAD, ALU.subtract,
                                                ALU.mult).then_inc(s_step, 1)
                        dve.wait_ge(s_step, 3 * n + 1)
                        dve.wait_ge(s_sg, n + 1)
                        silu_rest(a_t[:], bank[0][:, 0:P], b1_sb[:], sg[:]).then_inc(s_a, 1)
                        dve.wait_ge(s_y, n + 1)
                        nc.vector.scalar_tensor_tensor(e_t[:], bank[1][:, 0:P], GRAD, v_now[:], ALU.mult,
                                                       ALU.subtract).then_inc(s_e, 1)
                        dve.wait_ge(s_a, n + 1)
                        nc.vector.scalar_tensor_tensor(slope_u[:], sg[:], 1.0, a_t[:], ALU.subtract,
                                                       ALU.mult).then_inc(s_step, 1)
                        dve.wait_ge(s_step, 3 * n + 2)
                        nc.vector.tensor_tensor(slope[:], sg[:], slope_u[:], ALU.subtract).then_inc(s_slope, 1)
                        dve.wait_ge(s_eT, n + 1)
                        nc.vector.tensor_scalar(ed_rows[:, 0, 0, :], bank[6][:, 0:P], own, None,
                                                ALU.mult).then_inc(s_ed, 1)
                        dve.wait_ge(s_da, n + 1)
                        dve.wait_ge(s_sloperows, n + 1)
                        nc.vector.tensor_tensor(ed_rows[:, 1, 1, :], bank[2][:, 0:P], slope_rows[:],
                                                ALU.mult).then_inc(s_step, 1)
                        dve.wait_ge(s_step, 3 * n + 3)
                        nc.vector.tensor_scalar(ed_rows[:, 0, 1, :], ed_rows[:, 1, 1, :], own, None,
                                                ALU.mult).then_inc(s_ed, 1)
                        update(((w2_sb[:], bank[3][:, 0:P], n + 2), (w2t_sb[:], bank[4][:, 0:P], n + 2),
                                (b2_sb[:], bank[6][:, 0:1], n + 2), (w1_sb[:], bank[0][:, 0:P], n + 2),
                                (b1_sb[:], bank[5][:, 0:1], n + 2)), s_params)
                dve.wait_ge(s_params, 5 * S + 1)

            for g in range(NG):
                add_out_rows(dve, g, g)
                dve.wait_ge(res_done, g + 2)
                if g:
                    norm_moments(dve, at, g - 1, stats_there)
                stats_there = norm_stats(dve, at, g)
            norm_moments(dve, at, NG - 1, stats_there)
            normalise(dve, at)
            route(dve, at, 1)
            def ffn_group(g, first, last):
                def rest_of_transposed(k):
                    dve.wait_ge(xsT_hi, g * (E + 1) + (k + 1))
                    nc.vector.tensor_tensor(xs_lo[:, xs_buf(k), :], bank[4][:], xs_hi[:, xs_buf(k), :].bitcast(F32),
                                            ALU.subtract).then_inc(xsT_lo, 1)

                def low(m):
                    dve.wait_ge(sq_done, g * NHID + (m + 1 + BUFS))
                    dve.wait_ge(hi_done, g * NHID + (m + 1))
                    dve.wait_ge(out_mm_done, g * NHID + (m + 1))
                    nc.vector.tensor_tensor(hid_lo[:, m % BUFS, :], sq[:, m % BUFS, :],
                                            hid_hi[:, m % BUFS, :].bitcast(F32),
                                            ALU.subtract).then_inc(lo_even_done, 1)

                if first:
                    rest_of_transposed(0)
                for m in range(NHID):
                    k, j = divmod(m, FJ)
                    dve.wait_ge(relu_done, g * NHID + (m + 1 + BUFS))
                    if m >= BUFS or not first:
                        dve.wait_ge(lo_even_done if m % 2 else lo_odd_done, g * (NHID // 2) + ((m - BUFS) // 2 + 1))
                    nc.vector.tensor_tensor(sq[:, m % BUFS, :], relu[:, m % BUFS, :], relu[:, m % BUFS, :],
                                            ALU.mult).then_inc(sq_done, 1)
                    if m % 2:
                        low(m - 1)
                    if j == 1 and not (k == E and last):
                        rest_of_transposed(k + 1)
                    if m == BUFS + 2 and not first:
                        add_out_rows(dve, g + (NG - 1), g - 1)
                if last:
                    add_out_rows(dve, g + NG, g)

            ffn_groups(dve, ffn_group)

        @block.tensor
        def _(pe):
            pe.sem_inc(out_mm_done, BUFS)
            pe.sem_inc(xsT_done, 2)
            for starts_at_1 in (out_rows_done, upd_done, s_upd):
                pe.sem_inc(starts_at_1, 1)
            pe.wait_ge(consts_made, 2 + B)
            pe.wait_ge(weights_in, 16)
            pe.sem_inc(p_out_mm_done, PBUFS)
            pe.sem_inc(p_xsT_done, 2)

            def queries(u):
                if u >= 2:
                    pe.wait_ge(q_copied, u - 1)
                nc.tensor.matmul(bank[4 + u % 2][:, 0:PCOLS], wq_sb[:], ln_t[:, u * PCOLS:(u + 1) * PCOLS],
                                 start=True, stop=True).then_inc(q_done, 1)

            def scan_pair(b, n):
                def side(t, *slots):
                    if n is None:
                        if slots[0] == 3 and t - 2 in range(T // PCOLS):
                            queries(t - 2)
                        return
                    pe_fill(pe, n, [5 * t + s for s in slots])
                    for part in {(PASSES - 4, 2): ("out",), (PASSES - 1, 1): ("ln",)}.get((t, slots[0]), ()):
                        pe_next(pe, n, part)

                for q in range(PAIR):
                    c = b * PAIR + q
                    for i in range(ITERS):
                        n1 = c * ITERS + (i + 1)
                        t = q * ITERS + i
                        old = buf(i - 1)
                        if i == 0:
                            pe.wait_ge(params_done, 5 * c + 1)
                            mm(bank[0], w1_sb[:], k_t[:, col(c)]).then_inc(h_done, 1)
                            if q == 0:
                                pe_next(pe, b, "kk")
                        else:
                            pe.wait_ge(aa_done, c * (ITERS - 1) + i)
                            if i == 1:
                                pe.wait_ge(round_act, 2 * c + 2)
                                pe.wait_ge(round_dve, 3 * c + 1)
                            if coarse(i):
                                mm(bank[0], w1_r[:], k_r[:], stop=False)
                            else:
                                mm(bank[0], w1_sb[:], k_t[:, col(c)], stop=False)
                            pe.wait_ge(d_done, c * ITERS + i)
                            if t == 1:
                                pe.wait_ge(kk_done, b + 1)
                            kk_now = kk_r[:] if coarse(i) else kk[:, bass.ds(c, 1), :].rearrange("p a d -> p (a d)")
                            mm(bank[0], kind(ed_rows, ed_rows_r, i)[:, old, 1, :], kk_now,
                               start=False).then_inc(h_done, 1)
                            pe.wait_ge(ee_done, c * (ITERS - 1) + i)
                            pe.wait_ge(erows_done, c * ITERS + i)
                            mm(bank[1], kind(ed_rows, ed_rows_r, i)[:, old, 0, :], kind(aa, aa_r, i)[:], stop=False)
                        side(t, 0)
                        pe.wait_ge(a_done, n1)
                        if i == 0:
                            pe.wait_ge(params_done, 5 * c + 4)
                        a_now, e_now = kind(a_t, a_r, i)[:], kind(e_t, e_r, i)[:]
                        if i == 1:
                            pe.wait_ge(round_dve, 3 * c + 3)
                        mm(bank[1], kind(w2_sb, w2_r, i)[:], a_now, start=(i == 0)).then_inc(y_done, 1)
                        nc.tensor.transpose(bank[3][:, 0:P], a_now.bitcast(F32), ident[:])
                        pe.wait_ge(th_done, n1)
                        nc.tensor.transpose(bank[3][:, P:2 * P], th[:], ident[:]).then_inc(athT_done, 1)
                        if i < ITERS - 1:
                            mm(bank[0], a_now, a_now).then_inc(aa_mm_done, 1)
                        side(t, 1)
                        pe.wait_ge(arows_done, n1)
                        if i:
                            mm(bank[2], kind(ee, ee_r, i)[:], kind(a_rows, a_rows_r, i)[:], stop=False)
                        side(t, 2)
                        pe.wait_ge(e_done, n1)
                        mm(bank[2], e_now, kind(w2t_sb, w2t_r, i)[:], start=(i == 0)).then_inc(da_done, 1)
                        if i < ITERS - 1:
                            mm(bank[1], e_now, e_now).then_inc(ee_mm_done, 1)
                        pe.wait_ge(slope_step, n1)
                        nc.tensor.transpose(bank[3][:, 2 * P:3 * P], e_now.bitcast(F32), ident[:]).then_inc(eT_done, 1)
                        if i < ITERS - 1:
                            side(t, 3, 4)
                    if n is not None and q == PAIR - 1:
                        pe_next(pe, n, "k")
                    side(q * ITERS + ITERS - 1, 3)
                    e_last, d_last = (ed_rows[:, buf(ITERS - 1), k, :] for k in range(2))
                    pe.wait_ge(know_done, c + 1)
                    pe.wait_ge(d_done, (c + 1) * ITERS)
                    mm(bank[0], krow_now[:], d_last).then_inc(upd_done, 1)
                    nc.tensor.matmul(bank[0][:, P:P + 1], d_last, ones[:, 0:1], start=True, stop=True)\
                      .then_inc(upd_done, 1)
                    pe.wait_ge(erows_done, (c + 1) * ITERS)
                    mm(bank[3], a_rows[:], e_last).then_inc(upd_done, 1)
                    nc.tensor.matmul(bank[3][:, P:P + 1], e_last, ones[:, 0:1], start=True, stop=True)\
                      .then_inc(upd_done, 1)
                    mm(bank[1], e_last, a_rows[:]).then_inc(upd_done, 1)
                    if n is not None and q == PAIR - 1:
                        pe_next(pe, n, "v")
                    side(q * ITERS + ITERS - 1, 4)

            pe_route(pe, 0)
            pe_fill(pe, 0, range(FILL), first=True)
            pe.wait_ge(params_in, 16 * 7)
            for part in ("out", "ln", "k", "v"):
                pe_next(pe, 0, part)
            pe.wait_ge(params_in, 16 * 7)
            with pe.Fori(0, NPAIR - 1) as b:
                pe.wait_ge(kcopy_done, b + 1)
                scan_pair(b, b + 1)
            pe.wait_ge(kcopy_done, NPAIR)
            scan_pair(NPAIR - 1, None)

            pe.wait_ge(gap_done, NBLK + 1)
            nc.tensor.matmul(bank[7][0:1, 0:4], ones[:, 0:1], norms[:], start=True, stop=True).then_inc(total_done, 1)
            pe.wait_ge(flag_done, 1)
            ok = pe.value_load(flag[0:1, 0:1], min_val=0, max_val=1)
            with pe.If(ok == 0):
                pe.wait_ge(params_in, 16 * 12)
                with pe.Fori(0, NBLK) as c:
                    with pe.Fori(0, STEPS) as t:
                        pe.wait_ge(s_know, c + 1)
                        n = c * STEPS + t
                        pe.wait_ge(s_params, 5 * n + 1)
                        mm(bank[0], w1_sb[:], k_t[:, col(c)]).then_inc(s_h, 1)
                        pe.wait_ge(s_a, n + 1)
                        mm(bank[1], w2_sb[:], a_t[:]).then_inc(s_y, 1)
                        nc.tensor.transpose(bank[5][:, 0:P], a_t[:], ident[:]).then_inc(s_aT, 1)
                        pe.wait_ge(s_e, n + 1)
                        mm(bank[2], e_t[:], w2t_sb[:]).then_inc(s_da, 1)
                        nc.tensor.transpose(bank[6][:, 0:P], e_t[:], ident[:]).then_inc(s_eT, 1)
                        pe.wait_ge(s_slope, n + 1)
                        nc.tensor.transpose(bank[7][:, 0:P], slope[:], ident[:]).then_inc(s_slopeT, 1)
                        pe.wait_ge(s_arows, n + 1)
                        pe.wait_ge(s_ed, 2 * n + 2)
                        mm(bank[3], a_rows[:], ed_rows[:, 0, 0, :])
                        mm(bank[4], ed_rows[:, 0, 0, :], a_rows[:])
                        nc.tensor.matmul(bank[6][:, 0:1], ed_rows[:, 0, 0, :], ones[:, 0:1], start=True, stop=True)
                        mm(bank[0], krow_now[:], ed_rows[:, 0, 1, :])
                        nc.tensor.matmul(bank[5][:, 0:1], ed_rows[:, 0, 1, :], ones[:, 0:1], start=True,
                                         stop=True).then_inc(s_upd, 1)
                pe.wait_ge(s_params, 5 * S + 1)

            pe.wait_ge(q_copied, T // PCOLS)
            for g in range(NG):
                nc.tensor.matmul(bank[g][:], w1_sb[:], ln_t[:, g * COLS:(g + 1) * COLS],
                                 start=True, stop=True).then_inc(qh_done, 1)
            for g in range(NG):
                pe.wait_ge(qa_done, g + 1)
                nc.tensor.matmul(bank[QY_BANK[g]][:], w2_sb[:], q_hid[g], start=True, stop=True).then_inc(qy_done, 1)
                if g:
                    pe_out_rows(pe, g - 1, q_out[:, (g - 1) % 2, :])
            pe_out_rows(pe, NG - 1, q_out[:, (NG - 1) % 2, :])
            pe_route(pe, 1)
            ffn_groups(pe, lambda g, first, last: pe_ffn_group(pe, g, first, last))


def kernel(**inputs):
    import numpy as np
    import concourse.bacc as bacc
    from concourse.bass_utils import run_bass_kernel_spmd

    a = {n: np.asarray(v) for n, v in inputs.items()}
    fc = np.concatenate([a["L0_ffn_shared_fc"][None], a["L0_ffn_w_fc"]], 0)
    proj = np.concatenate([a["L0_ffn_shared_proj"][None], a["L0_ffn_w_proj"]], 0)
    arrays = {
        "x": a["L0_attn_x"],
        "wq": a["L0_attn_W_Q"],
        "wkv": a["L0_attn_W_KV"],
        "w1": a["L0_attn_W1"],
        "b1": a["L0_attn_b1"],
        "w2": a["L0_attn_W2"],
        "w2t": a["L0_attn_W2"].T,
        "b2": a["L0_attn_b2"],
        "router": a["L0_ffn_router_w"].T,
        "experts": np.stack([fc.transpose(2, 0, 1),
                             proj.reshape(E + 1, P, FJ, P).transpose(3, 0, 2, 1).reshape(P, E + 1, FJ * P)], 2),
    }
    arrays = {n: np.ascontiguousarray(v) for n, v in arrays.items()}
    nc = bacc.Bacc("TRN2", target_bir_lowering=False, num_devices=1)
    args = {n: nc.dram_tensor(n, v.shape, mybir.dt.from_np(v.dtype), kind="ExternalInput").ap()
            for n, v in arrays.items()}
    out = nc.dram_tensor("out", (B, S, P), F32, kind="ExternalOutput").ap()
    mk_macaron(nc, out=out, **args)
    r = run_bass_kernel_spmd(nc, [arrays], core_ids=[0])
    return r.results[0]["out"]
```
